# Optimizing a Trainium2 kernel written in Bass

```python
import numpy as np
import jax
import jax.numpy as jnp

def _softmax(x, axis=-1):
    return jax.nn.softmax(x, axis=axis)

def _gelu(x):
    return jax.nn.gelu(x, approximate=True)

def _silu(x):
    return jax.nn.silu(x)

def _sigmoid(x):
    return jax.nn.sigmoid(x)

def _layernorm(x, axis=-1, eps=1e-05):
    m = jnp.mean(x, axis=axis, keepdims=True)
    v = jnp.var(x, axis=axis, keepdims=True)
    return (x - m) / jnp.sqrt(v + eps)

def _scatter_add(tgt, idx, src, axis=0):
    return tgt.at[idx].add(src)

def _segment_sum(src, seg, n):
    return jax.ops.segment_sum(src, seg, n)
kernel_name = 'mk_adj_preln_d2_adj_r2_d778f5'

def setup_inputs(seed: int=0):
    np.random.seed(seed)
    _w = jnp.asarray

    def _rec_inputs():
        import jax
        import jax.numpy as jnp
        _gk = jax.random.key(seed)
        x = -9.806e-05 + 1 * jax.random.normal(jax.random.fold_in(_gk, 1), (8, 1024, 64), jnp.float32)
        _w = (1.0 + jnp.arange(1024, dtype=jnp.float32)) ** (-0.5)
        _w = _w / _w.mean()
        _pij = jnp.clip(0.015625 * _w[:, None] * _w[None, :], 0.0, 1.0)
        _a = jax.random.uniform(jax.random.fold_in(_gk, 2), (8, 1024, 1024)) < _pij
        _af = _a.astype(jnp.float32)
        adj = _af
        _nm = jnp.ones((8, 1024), dtype=bool)
        nodemask = _nm
        return (x, adj, nodemask)
    x, adj, nodemask = _rec_inputs()

    def _L0_gnn_setup():
        import jax, jax.numpy as jnp
        import numpy as np
        B, N, DIM, H = (8, 512, 64, 8)
        SCALE = DIM ** (-0.5)
        key = jax.random.key(seed)
        ks = jax.random.split(key, 6)
        x = jax.random.normal(ks[0], (B, N, DIM), dtype=jnp.float32)
        adj = (jax.random.uniform(ks[1], (B, N, N)) < 0.05).astype(jnp.float32)
        W_qkv = jax.random.normal(ks[2], (3 * H * DIM, DIM), dtype=jnp.float32) * DIM ** (-0.5)
        W_proj = jax.random.normal(ks[3], (DIM, H * DIM), dtype=jnp.float32) * (H * DIM) ** (-0.5)
        b_proj = jnp.zeros((DIM,), dtype=jnp.float32)
        W_gamma = jax.random.uniform(ks[4], (2, DIM), dtype=jnp.float32) * 0.01
        b_gamma = jnp.zeros((2,), dtype=jnp.float32)
        return {'x': x, 'adj': adj, 'W_qkv': W_qkv, 'W_proj': W_proj, 'b_proj': b_proj, 'W_gamma': W_gamma, 'b_gamma': b_gamma}
    _L0_gnn_all = _L0_gnn_setup()
    _L0_gnn_in = {k: v for k, v in _L0_gnn_all.items() if k in ('W_qkv', 'W_proj', 'b_proj', 'W_gamma', 'b_gamma')}
    del _L0_gnn_all

    def _L1_gnn_setup():
        import jax, jax.numpy as jnp
        import numpy as np
        B, N, C, H = (8, 256, 64, 128)
        T, K = (10, 2)
        TAUS = (0.25, 0.5, 0.75)
        WTS = (0.25, 0.5, 0.25)
        EPS_GIN = 0.0
        AVG_DEG = 32.0
        key = jax.random.key(seed)
        ks = jax.random.split(key, 6)
        x = jax.random.normal(ks[0], (B, N, C), jnp.float32)
        u = jax.random.uniform(ks[1], (B, N, N))
        a = u < AVG_DEG / N
        adj = jnp.maximum(a, jnp.swapaxes(a, 1, 2)).astype(jnp.float32)
        mask = jax.random.bernoulli(ks[2], 0.9, (B, N))
        W1 = jax.random.normal(ks[3], (C, H), jnp.float32) / np.float32(np.sqrt(C))
        b1 = jnp.zeros((H,), jnp.float32)
        W2 = jax.random.normal(ks[4], (H, C), jnp.float32) / np.float32(np.sqrt(H))
        b2 = jnp.zeros((C,), jnp.float32)
        return {'x': x, 'adj': adj, 'mask': mask, 'W1': W1, 'b1': b1, 'W2': W2, 'b2': b2}
    _L1_gnn_all = _L1_gnn_setup()
    _L1_gnn_in = {k: v for k, v in _L1_gnn_all.items() if k in ('W1', 'b1', 'W2', 'b2')}
    del _L1_gnn_all
    return {'x': x, 'adj': adj, 'nodemask': nodemask, 'L0_gnn_W_qkv': _L0_gnn_in['W_qkv'], 'L0_gnn_W_proj': _L0_gnn_in['W_proj'], 'L0_gnn_b_proj': _L0_gnn_in['b_proj'], 'L0_gnn_W_gamma': _L0_gnn_in['W_gamma'], 'L0_gnn_b_gamma': _L0_gnn_in['b_gamma'], 'L1_gnn_W1': _L1_gnn_in['W1'], 'L1_gnn_b1': _L1_gnn_in['b1'], 'L1_gnn_W2': _L1_gnn_in['W2'], 'L1_gnn_b2': _L1_gnn_in['b2']}

def reference(x, adj, nodemask, L0_gnn_W_qkv, L0_gnn_W_proj, L0_gnn_b_proj, L0_gnn_W_gamma, L0_gnn_b_gamma, L1_gnn_W1, L1_gnn_b1, L1_gnn_W2, L1_gnn_b2):
    import jax
    import jax.numpy as jnp

    def _L0_gnn_ref(x, adj, W_qkv, W_proj, b_proj, W_gamma, b_gamma):
        import jax, jax.numpy as jnp
        import numpy as np
        B, N, DIM, H = (8, 512, 64, 8)
        SCALE = DIM ** (-0.5)
        b, n, c = x.shape
        qkv = jnp.einsum('bnc,kc->bnk', x, W_qkv)
        qkv = qkv.reshape(b, n, 3, H, DIM).transpose(0, 3, 1, 2, 4)
        q, k, v = (qkv[..., 0, :], qkv[..., 1, :], qkv[..., 2, :])
        attn = jnp.einsum('bhnd,bhmd->bhnm', q, k) * SCALE
        gamma = jnp.exp(x @ W_gamma.T + b_gamma)
        g0 = gamma[:, None, :, 0:1]
        g1 = gamma[:, None, :, 1:2]
        attn = g0 * attn + g1 * adj[:, None]
        attn = jax.nn.softmax(attn, axis=-1)
        out = jnp.einsum('bhnm,bhmd->bnhd', attn, v).reshape(b, n, H * DIM)
        return out @ W_proj.T + b_proj

    def _L1_gnn_ref(x, adj, mask, W1, b1, W2, b2):
        import jax, jax.numpy as jnp
        import numpy as np
        B, N, C, H = (8, 256, 64, 128)
        T, K = (10, 2)
        TAUS = (0.25, 0.5, 0.75)
        WTS = (0.25, 0.5, 0.25)
        EPS_GIN = 0.0
        AVG_DEG = 32.0
        Bc, Nc, Cc = x.shape
        eye = jnp.eye(Nc, dtype=bool)
        adj_ = jnp.where(eye, 1.0, adj)
        neigh = (adj_ > 0) & ~eye
        ni = neigh.astype(jnp.int32)
        rank = jnp.cumsum(ni, axis=-1) - ni
        nb = ni.sum(-1)
        skip = jnp.where(nb > T, (nb + K - 1) // K, 1)
        skip = jnp.maximum(skip, 1)
        sk = skip[:, :, None]
        rem = neigh & (sk > 1) & (rank % sk == sk - 1) & mask[:, :, None]
        rem = rem | jnp.swapaxes(rem, 1, 2)
        adj_d = jnp.where(rem, 0.0, adj_)
        nd = adj_d > 0
        vals = jnp.where(nd[..., None], x[:, None, :, :], jnp.inf)
        s = jnp.sort(vals, axis=2)
        nv = nd.sum(2)
        agg = jnp.zeros_like(x)
        for tau, w in zip(TAUS, WTS):
            pos = jnp.asarray(tau, x.dtype) * jnp.maximum(nv - 1, 0).astype(x.dtype)
            lo = jnp.floor(pos).astype(jnp.int32)
            hi = jnp.ceil(pos).astype(jnp.int32)
            frac = (pos - lo.astype(x.dtype))[..., None]
            idx_lo = jnp.broadcast_to(lo[:, :, None, None], (Bc, Nc, 1, Cc))
            idx_hi = jnp.broadcast_to(hi[:, :, None, None], (Bc, Nc, 1, Cc))
            v_lo = jnp.take_along_axis(s, idx_lo, axis=2)[:, :, 0, :]
            v_hi = jnp.take_along_axis(s, idx_hi, axis=2)[:, :, 0, :]
            agg = agg + jnp.asarray(w, x.dtype) * (v_lo + frac * (v_hi - v_lo))
        agg = jnp.where(nv[..., None] > 0, agg, 0.0)
        out = (1.0 + EPS_GIN) * x + agg
        h = jax.nn.relu(out @ W1 + b1)
        y = h @ W2 + b2
        return y * mask[..., None].astype(y.dtype)
    h = jnp.maximum(_layernorm(x, axis=-1), 0.0)
    x = x + _L0_gnn_ref(h, adj, L0_gnn_W_qkv, L0_gnn_W_proj, L0_gnn_b_proj, L0_gnn_W_gamma, L0_gnn_b_gamma)
    h = jnp.maximum(_layernorm(x, axis=-1), 0.0)
    x = x + _L1_gnn_ref(h, adj, nodemask, L1_gnn_W1, L1_gnn_b1, L1_gnn_W2, L1_gnn_b2)
    return x

_drawn_inputs = setup_inputs


def setup_inputs(seed=0):
    import zlib

    import numpy as np

    out = dict(_drawn_inputs(seed))
    spreads = {'L0_gnn_b_proj': (0.0, 0.1),
     'L0_gnn_b_gamma': (0.0, 0.8),
     'L1_gnn_b1': (0.0, 0.1),
     'L1_gnn_b2': (0.0, 0.1)}
    factors = {'L0_gnn_W_gamma': 8.0}
    for name, (base, spread) in spreads.items():
        noise = np.random.default_rng([zlib.crc32(name.encode()), seed]).standard_normal(out[name].shape)
        drawn = base * np.exp(spread * noise) if base else spread * noise
        out[name] = jnp.asarray(drawn.astype(out[name].dtype))
    for name, factor in factors.items():
        out[name] = (out[name] * factor).astype(out[name].dtype)
    return out
```

```python
import concourse.bass as bass
from concourse import mybir
from contextlib import ExitStack

FP32 = mybir.dt.float32
BF16 = mybir.dt.bfloat16
FP16 = mybir.dt.float16
INT32 = mybir.dt.int32
UINT8 = mybir.dt.uint8
ALU = mybir.AluOpType
ACT = mybir.ActivationFunctionType
AX = mybir.AxisListType

P = 128
BANK = 512


class Shapes:

    def __init__(self, x, w_qkv, w1):
        self.B, self.N, self.C = x.shape
        self.T = self.N // P
        self.F = w_qkv.shape[0] // 3
        self.D = self.C
        self.H = self.F // self.D
        self.HP = self.H // 2
        self.HID = w1.shape[1]


TAUS = (0.25, 0.5, 0.75)
WTS = (0.25, 0.5, 0.25)
DEG_T = 10.0
EPS = 1e-5


def wait_alone(eng, sem, value, passed):
    eng.wait_ge(sem, value)
    eng.sem_inc(passed, 1)


def layer_norm_relu(nc, x, h, tmp, mean, var, y, t):
    v = nc.vector
    G, C = x.shape[1], x.shape[2]
    v.reduce_sum(mean, x, axis=AX.X)
    v.drain()
    v.tensor_scalar(mean, mean, 1.0 / C, None, ALU.mult)
    v.drain()
    v.tensor_tensor(h, x, mean[:, :, None].to_broadcast([P, G, C]), ALU.subtract)
    v.drain()
    v.tensor_tensor(tmp, h, h, ALU.mult)
    v.drain()
    v.reduce_sum(var, tmp, axis=AX.X)
    v.drain()
    v.tensor_scalar(var, var, 1.0 / C, EPS, ALU.mult, ALU.add)
    v.drain()
    v.tensor_scalar(t.bitcast(INT32), var.bitcast(INT32), 1, None, ALU.logical_shift_right)
    v.drain()
    v.tensor_scalar(y.bitcast(INT32), t.bitcast(INT32), -1.0, 1597463007.0, ALU.mult, ALU.add)
    v.drain()
    for _ in range(4):
        v.tensor_tensor(t, y, y, ALU.mult)
        v.drain()
        v.tensor_tensor(t, t, var, ALU.mult)
        v.drain()
        v.tensor_scalar(t, t, -0.5, 1.5, ALU.mult, ALU.add)
        v.drain()
        v.tensor_tensor(y, y, t, ALU.mult)
        v.drain()
    v.tensor_tensor(tmp, h, y[:, :, None].to_broadcast([P, G, C]), ALU.mult)
    v.drain()
    return v.tensor_scalar(h, tmp, 0.0, None, ALU.max)


def setup_phase(nc, S, d, sb):
    with ExitStack() as ctx:
        buf = lambda n, s, dt=FP32: ctx.enter_context(nc.sbuf_tensor(n, s, dt))
        sem = lambda n: ctx.enter_context(nc.semaphore(n))
        KT = 3 * S.F // P
        wqkv_rows = buf("wqkv_rows", [P, KT, S.C])
        wproj_rows = buf("wproj_rows", [S.C, S.F])
        wgam_rows = buf("wgam_rows", [2, S.C])
        mask_rows = buf("mask_rows", [S.B * S.T, P], UINT8)
        mask_rows_f = buf("mask_rows_f", [S.B * S.T, P])
        tmp = buf("ln_tmp0", [P, S.T * S.B, S.C])
        mean, var, y, t = (buf(f"ln0_{n}", [P, S.T * S.B]) for n in ("mean", "var", "y", "t"))
        ps = ctx.enter_context(nc.psum_tensor("ps_setup", [P, 8 * BANK], FP32))
        loaded_x, loaded_w, ident_done, ones_done = sem("su_x"), sem("su_w"), sem("su_id"), sem("su_one")
        copied, turned = sem("su_copied"), sem("su_turned")
        block = ctx.enter_context(nc.Block())

        @block.sync
        def _(sp):
            for b in range(S.B):
                sp.dma_start(sb["x1"][:, :, b, :], d["x"][b].rearrange("(t p) c -> p t c", p=P)).then_inc(loaded_x, 16)

        @block.scalar
        def _(act):
            for dst, src in (
                (wqkv_rows[:], d["w_qkv"].rearrange("(t p) c -> p t c", p=P)),
                (wproj_rows[:], d["w_proj"]),
                (wgam_rows[:], d["w_gamma"]),
                (mask_rows[:], d["mask"].rearrange("b (t p) -> (b t) p", p=P)),
                (sb["bproj"][:], d["b_proj"][None, :].to_broadcast([P, S.C])),
                (sb["bgam"][:], d["b_gamma"][None, :].to_broadcast([P, 2])),
                (sb["w1"][:], d["w1"]),
                (sb["b1"][:], d["b1"][:, None]),
                (sb["w2"][:], d["w2"]),
                (sb["b2"][:], d["b2"][None, :].to_broadcast([P, S.C])),
            ):
                act.dma_start(dst, src).then_inc(loaded_w, 16)

        @block.gpsimd
        def _(pool):
            nc.gpsimd.memset(sb["ident"][:], 0.0)
            nc.gpsimd.memset(sb["ones"][:], 1.0).then_inc(ones_done, 1)
            pool.wait_ge(ones_done, 1)
            nc.gpsimd.affine_select(out=sb["ident"][:], in_=sb["ident"][:], compare_op=ALU.not_equal, fill=1.0,
                                    base=0, pattern=[[-1, P]], channel_multiplier=1).then_inc(ident_done, 1)

        @block.tensor
        def _(pe):
            pe.wait_ge(loaded_w, 160)
            pe.wait_ge(ident_done, 1)
            for k in range(KT):
                nc.tensor.transpose(ps[0:S.C, k * P:(k + 1) * P], wqkv_rows[:, k, :], sb["ident"][:])
            for k in range(S.F // P):
                nc.tensor.transpose(ps[:, 3 * BANK + k * S.C:3 * BANK + (k + 1) * S.C],
                                    wproj_rows[:, k * P:(k + 1) * P], sb["ident"][0:S.C, 0:S.C])
            nc.tensor.transpose(ps[0:S.C, 5 * BANK:5 * BANK + 2], wgam_rows[:], sb["ident"][0:2, 0:2])
            pe.wait_ge(copied, 1)
            nc.tensor.transpose(ps[:, 4 * BANK:4 * BANK + S.B * S.T], mask_rows_f[:],
                                sb["ident"][0:S.B * S.T, 0:S.B * S.T]).then_inc(turned, 1)

        @block.vector
        def _(v):
            v.wait_ge(loaded_w, 160)
            nc.vector.tensor_copy(mask_rows_f[:], mask_rows[:]).then_inc(copied, 1)
            v.wait_ge(ident_done, 1)
            nc.vector.tensor_copy(sb["ident_b"][:], sb["ident"][:])
            nc.vector.tensor_copy(sb["ones_b"][:], sb["ones"][:, 0:1])
            nc.vector.tensor_scalar(sb["off_diag"][:], sb["ident"][:], -1.0, 1.0, ALU.mult, ALU.add)
            v.wait_ge(loaded_x, 16 * S.B)
            layer_norm_relu(nc, sb["x1"][:].rearrange("p t b c -> p (t b) c"), sb["h"][:].rearrange("p t b c -> p (t b) c"),
                            tmp[:], mean[:], var[:], y[:], t[:])
            v.wait_ge(turned, 1)
            nc.vector.tensor_scalar(sb["wqkvT"][:, 0:S.F], ps[0:S.C, 0:S.F], S.D ** -0.5, None, ALU.mult)
            nc.vector.tensor_copy(sb["wqkvT"][:, S.F:], ps[0:S.C, S.F:3 * S.F])
            nc.vector.tensor_copy(sb["wprojT"][:].rearrange("p k c -> p (k c)"),
                                  ps[:, 3 * BANK:3 * BANK + S.F // P * S.C])
            nc.vector.tensor_copy(sb["wgam"][:], ps[0:S.C, 5 * BANK:5 * BANK + 2])
            nc.vector.tensor_copy(sb["wgam0"][:], ps[0:S.C, 5 * BANK:5 * BANK + 1].to_broadcast([S.C, P]))
            nc.vector.tensor_copy(sb["mask"][:], ps[:, 4 * BANK:4 * BANK + S.B * S.T])


def attention_phase(nc, S, d, sb):
    with ExitStack() as ctx:
        buf = lambda n, s, dt=FP32: ctx.enter_context(nc.sbuf_tensor(n, s, dt))
        sem = lambda n: ctx.enter_context(nc.semaphore(n))
        h_b = buf("h_b", [P, S.T, S.C])
        hT = buf("hT", [S.C, S.N])
        g0 = buf("g0", [P, S.N])
        g1 = buf("g1", [P, S.T])
        kT = buf("kT", [P, S.HP, S.N])
        vals = buf("vals", [P, S.T, S.F])
        adj_t = [buf(f"adj_t{u}", [P, S.N]) for u in range(2)]
        bias_t = [buf(f"bias_t{u}", [P, S.N]) for u in range(2)]
        qT = [buf(f"qT{u}", [P, S.HP, P]) for u in range(2)]
        neg = [buf(f"neg{u}", [P, S.N]) for u in range(2)]
        prob = [buf(f"prob{u}", [P, S.N]) for u in range(2)]
        probT = [buf(f"probT{u}", [P, S.T, P]) for u in range(2)]
        neg_max = [buf(f"neg_max{u}", [P, S.H]) for u in range(2)]
        row_sum = [buf(f"row_sum{u}", [P, S.H]) for u in range(2)]
        row_inv = buf("row_inv", [P, S.H])
        o_sb = buf("o_sb", [P, S.F])
        oT = buf("oT", [P, S.F // P, P])
        y_sb = buf("y_sb", [P, S.C])
        ps = ctx.enter_context(nc.psum_tensor("ps_att", [P, 8 * BANK], FP32))
        bank = lambda k, n=1: ps[:, k * BANK:(k + n) * BANK]
        PT0, OB, MB = 4, 6, 7

        adj_ready = [sem(f"adj_ready{u}") for u in range(2)]
        adj_free = sem("adj_free")
        h_ready, passed = sem("h_ready"), sem("passed")
        job_done, job_read_v, job_read_a = sem("job_done"), sem("job_read_v"), sem("job_read_a")
        q_done, q_read = sem("q_done"), sem("q_read")
        s_done, s_read = sem("s_done"), sem("s_read")
        p_done = sem("p_done")
        t_done, t_read_v, t_read_a = sem("t_done"), sem("t_read_v"), sem("t_read_a")
        pv_done, o_norm, oT_done, oT_read = sem("pv_done"), sem("o_norm"), sem("oT_done"), sem("oT_read")
        y_done, tile_done = sem("y_done"), sem("tile_done")
        block = ctx.enter_context(nc.Block())

        HALVES = S.N // BANK
        K0 = 5
        V0 = K0 + S.HP * HALVES
        JOBS = V0 + S.T
        by_act = lambda j: j in (2, 3, 4) or (j >= K0 and j % 2 == 0)
        n_act = lambda j: sum(by_act(i) for i in range(j + 1))
        n_vec = lambda j: j + 1 - n_act(j)
        JA, JV = n_act(JOBS - 1), n_vec(JOBS - 1)

        @block.sync
        def _(sp):
            with sp.Fori(0, S.B) as b:
                with sp.Fori(0, S.T // 2) as i2:
                    for u in range(2):
                        n = b * S.T + i2 * 2 + u
                        sp.wait_ge(adj_free, n + 1)
                        sp.dma_start(adj_t[u][:], d["adj"][bass.ds(b, 1), bass.ds(i2 * (2 * P) + u * P, P), :]
                                     .rearrange("o p n -> (o p) n")).then_inc(adj_ready[u], 16)

        @block.tensor
        def _(pe):
            with pe.Fori(0, S.B) as b:
                wait_alone(pe, h_ready, b + 1, passed)
                for j in range(JOBS):
                    if j >= 8:
                        if by_act(j - 8):
                            pe.wait_ge(job_read_a, b * JA + n_act(j - 8))
                        else:
                            pe.wait_ge(job_read_v, b * JV + n_vec(j - 8))
                    if j < 2:
                        for k in range(BANK // P):
                            last = nc.tensor.transpose(bank(j)[0:S.C, k * P:(k + 1) * P],
                                                       h_b[:, j * (BANK // P) + k, :], sb["ident"][:])
                        last.then_inc(job_done, 1)
                        if j == 1:
                            pe.wait_ge(job_read_v, b * JV + 2)
                    elif j < 4:
                        nc.tensor.matmul(bank(j), sb["wgam0"][:], hT[:, (j - 2) * BANK:(j - 1) * BANK],
                                         start=True, stop=True).then_inc(job_done, 1)
                    elif j == 4:
                        for k in range(S.T):
                            last = nc.tensor.matmul(bank(j)[:, 2 * k:2 * k + 2], hT[:, k * P:(k + 1) * P],
                                                    sb["wgam"][:], start=True, stop=True)
                        last.then_inc(job_done, 1)
                    elif j < V0:
                        pair, half = divmod(j - K0, HALVES)
                        nc.tensor.matmul(bank(j % 8), sb["wqkvT"][:, S.F + pair * P:S.F + (pair + 1) * P],
                                         hT[:, half * BANK:(half + 1) * BANK],
                                         start=True, stop=True).then_inc(job_done, 1)
                    else:
                        k = j - V0
                        nc.tensor.matmul(bank(j % 8), hT[:, k * P:(k + 1) * P], sb["wqkvT"][:, 2 * S.F:3 * S.F],
                                         start=True, stop=True).then_inc(job_done, 1)
                with pe.Fori(0, S.T // 2) as i2:
                    pe.wait_ge(job_read_a, b * JA + JA)
                    pe.wait_ge(job_read_v, b * JV + JV)
                    for u in range(2):
                        n = b * S.T + i2 * 2 + u
                        pe.wait_ge(tile_done, n + 1)
                        for pair in range(S.HP):
                            last = nc.tensor.matmul(bank(MB)[:, pair * P:(pair + 1) * P],
                                                    sb["wqkvT"][:, pair * P:(pair + 1) * P],
                                                    hT[:, bass.ds(i2 * (2 * P) + u * P, P)], start=True, stop=True)
                        last.then_inc(q_done, 1)

                        def scores(h):
                            g = n * S.H + h
                            pe.wait_ge(s_read, g + 1)
                            r = (h % 2) * S.D
                            for half in range(HALVES):
                                last = nc.tensor.matmul(ps[:, (2 * (h % 2) + half) * BANK:(2 * (h % 2) + half + 1) * BANK],
                                                        qT[u][r:r + S.D, h // 2, :],
                                                        kT[r:r + S.D, h // 2, half * BANK:(half + 1) * BANK],
                                                        start=True, stop=True)
                            last.then_inc(s_done, 1)

                        def turn(h):
                            g = n * S.H + h
                            pe.wait_ge(p_done, g + 3)
                            for half in range(HALVES):
                                pe.wait_ge(t_read_a if half else t_read_v, g + 1)
                                for k in range(BANK // P):
                                    c = half * BANK + k * P
                                    last = nc.tensor.transpose(bank(PT0 + half)[:, k * P:(k + 1) * P],
                                                               prob[h % 2][:, c:c + P], sb["ident"][:])
                                last.then_inc(t_done, 1)

                        def weigh(h):
                            g = n * S.H + h
                            pe.wait_ge(t_read_a, g + 2)
                            pe.wait_ge(t_read_v, g + 2)
                            for k in range(S.T):
                                last = nc.tensor.matmul(bank(OB)[:, h * S.D:(h + 1) * S.D], probT[h % 2][:, k, :],
                                                        vals[:, k, h * S.D:(h + 1) * S.D],
                                                        start=(k == 0), stop=(k == S.T - 1))
                            last.then_inc(pv_done, 1)

                        pe.wait_ge(q_read, n + 1)
                        scores(0)
                        for h in range(S.H):
                            if h + 1 < S.H:
                                scores(h + 1)
                            turn(h)
                            if h:
                                weigh(h - 1)
                        weigh(S.H - 1)
                        pe.wait_ge(o_norm, n + 1)
                        for k in range(S.F // P):
                            last = nc.tensor.transpose(bank(MB)[:, k * P:(k + 1) * P], o_sb[:, k * P:(k + 1) * P],
                                                       sb["ident"][:])
                        last.then_inc(oT_done, 1)
                        pe.wait_ge(oT_read, n + 1)
                        for k in range(S.F // P):
                            last = nc.tensor.matmul(bank(MB)[:, 0:S.C], oT[:, k, :], sb["wprojT"][:, k, :],
                                                    start=(k == 0), stop=(k == S.F // P - 1))
                        last.then_inc(y_done, 1)

        @block.scalar
        def _(act):
            act.sem_inc(t_read_a, 1)
            act.sem_inc(p_done, 2)
            with act.Fori(0, S.B) as b:
                for j in range(JOBS):
                    if not by_act(j):
                        continue
                    act.wait_ge(job_done, b * JOBS + j + 1)
                    if j < 4:
                        i = nc.scalar.activation(g0[:, (j - 2) * BANK:(j - 1) * BANK], bank(j), ACT.Exp,
                                                 bias=sb["bgam"][:, 0:1])
                    elif j == 4:
                        i = nc.scalar.activation(g1[:], bank(j)[:, 1:2 * S.T:2], ACT.Exp, bias=sb["bgam"][:, 1:2])
                    elif j < V0:
                        pair, half = divmod(j - K0, HALVES)
                        i = nc.scalar.copy(kT[:, pair, half * BANK:(half + 1) * BANK], bank(j % 8))
                    else:
                        i = nc.scalar.copy(vals[:, j - V0, :], bank(j % 8))
                    i.then_inc(job_read_a, 1)
                with act.Fori(0, S.T // 2) as i2:
                    for u in range(2):
                        n = b * S.T + i2 * 2 + u

                        def exps(h):
                            g = n * S.H + h
                            act.wait_ge(s_read, g + 3)
                            act.wait_ge(t_done, g * 2 + 1)
                            nc.scalar.activation(prob[h % 2][:], neg[h % 2][:], ACT.Exp, scale=-1.0,
                                                 bias=neg_max[u][:, h:h + 1],
                                                 accum_out=row_sum[u][:, h:h + 1]).then_inc(p_done, 1)

                        def evac(h):
                            g = n * S.H + h
                            act.wait_ge(t_done, g * 2 + 2 + 3)
                            act.wait_ge(pv_done, g + 1)
                            nc.scalar.copy(probT[h % 2][:, S.T // 2:, :].rearrange("p t q -> p (t q)"),
                                           bank(PT0 + 1)).then_inc(t_read_a, 1)

                        exps(0)
                        for h in range(S.H):
                            if h + 1 < S.H:
                                exps(h + 1)
                            evac(h)

        @block.vector
        def _(v):
            v.sem_inc(t_read_v, 1)
            v.sem_inc(s_read, 2)
            v.sem_inc(tile_done, 1)
            v.sem_inc(adj_free, 2)
            v.sem_inc(t_done, 3)
            v.sem_inc(pv_done, 2)
            with v.Fori(0, S.B) as b:
                nc.vector.tensor_copy(h_b[:], sb["h"][:, :, bass.ds(b, 1), :].rearrange("p t o c -> p (t o) c")).then_inc(h_ready, 1)
                for j in range(JOBS):
                    if by_act(j):
                        continue
                    v.wait_ge(job_done, b * JOBS + j + 1)
                    if j < 2:
                        i = nc.vector.tensor_copy(hT[:, j * BANK:(j + 1) * BANK], bank(j)[0:S.C, :])
                    elif j < V0:
                        pair, half = divmod(j - K0, HALVES)
                        i = nc.vector.tensor_copy(kT[:, pair, half * BANK:(half + 1) * BANK], bank(j % 8))
                    else:
                        i = nc.vector.tensor_copy(vals[:, j - V0, :], bank(j % 8))
                    i.then_inc(job_read_v, 1)
                with v.Fori(0, S.T // 2) as i2:
                    v.wait_ge(job_read_a, b * JA + JA)
                    for u in range(2):
                        n = b * S.T + i2 * 2 + u
                        v.wait_ge(adj_ready[u], (b * (S.T // 2) + i2) * 16 + 16)
                        nc.vector.tensor_scalar(bias_t[u][:], adj_t[u][:], g1[:, bass.ds(i2 * 2 + u, 1)], None,
                                                ALU.mult).then_inc(adj_free, 1)
                        v.wait_ge(q_done, n + 1)
                        nc.vector.tensor_tensor(
                            qT[u][:], bank(MB).rearrange("p (h q) -> p h q", q=P),
                            g0[:, bass.ds(i2 * (2 * P) + u * P, P)][:, None, :].to_broadcast([P, S.HP, P]),
                            ALU.mult).then_inc(q_read, 1)
                        v.drain()

                        def take_max(h):
                            g = n * S.H + h
                            v.wait_ge(s_done, g + 1)
                            wait_alone(v, p_done, g + 1, passed)
                            nc.vector.tensor_tensor_reduce(
                                out=neg[h % 2][:], in0=ps[:, 2 * (h % 2) * BANK:(2 * (h % 2) + 2) * BANK],
                                in1=bias_t[u][:], scale=-1.0, scalar=3.0e38, op0=ALU.add, op1=ALU.min,
                                accum_out=neg_max[u][:, h:h + 1]).then_inc(s_read, 1)

                        def evac(h):
                            g = n * S.H + h
                            v.wait_ge(t_done, g * 2 + 1 + 3)
                            v.wait_ge(pv_done, g + 1)
                            nc.vector.tensor_copy(probT[h % 2][:, 0:S.T // 2, :].rearrange("p t q -> p (t q)"),
                                                  bank(PT0)).then_inc(t_read_v, 1)

                        take_max(0)
                        for h in range(S.H):
                            if h + 1 < S.H:
                                take_max(h + 1)
                            evac(h)
                        v.wait_ge(pv_done, n * S.H + S.H + 2)
                        nc.vector.reciprocal(row_inv[:], row_sum[u][:])
                        v.drain()
                        nc.vector.tensor_tensor(o_sb[:].rearrange("p (h d) -> p h d", d=S.D),
                                                bank(OB).rearrange("p (h d) -> p h d", d=S.D),
                                                row_inv[:, :, None].to_broadcast([P, S.H, S.D]),
                                                ALU.mult).then_inc(o_norm, 1)
                        v.wait_ge(oT_done, n + 1)
                        nc.vector.tensor_copy(oT[:].rearrange("p k q -> p (k q)"), bank(MB)).then_inc(oT_read, 1)
                        v.wait_ge(y_done, n + 1)
                        nc.vector.tensor_tensor(y_sb[:], bank(MB)[:, 0:S.C], sb["bproj"][:], ALU.add)
                        v.drain()
                        x1 = sb["x1"][:, bass.ds(i2 * 2 + u, 1), bass.ds(b, 1), :].rearrange("p t b c -> p (t b c)")
                        nc.vector.tensor_tensor(x1, x1, y_sb[:], ALU.add).then_inc(tile_done, 1)


def sort_phase(nc, S, d, sb):
    with ExitStack() as ctx:
        buf = lambda n, s, dt=FP32: ctx.enter_context(nc.sbuf_tensor(n, s, dt))
        sem = lambda n: ctx.enter_context(nc.semaphore(n))
        BP = S.B // 2
        tmp = buf("ln_tmp1", [P, S.T * S.B, S.C])
        mean, var, y, t = (buf(f"ln1_{n}", [P, S.T * S.B]) for n in ("mean", "var", "y", "t"))
        keys = [buf(f"keys{i}", [P, BP * S.N]) for i in range(2)]
        ps = ctx.enter_context(nc.psum_tensor("ps_sort", [P, 8 * BANK], FP32))
        normed, turned, copied_v, copied_a, is_sorted, stored = (
            sem(n) for n in ("so_normed", "so_turned", "so_copied_v", "so_copied_a", "so_sorted", "so_stored"))
        block = ctx.enter_context(nc.Block())
        levels = S.N.bit_length() - 1
        STEPS = levels * (levels + 1) // 2
        JOBS = BP * S.N // BANK
        PER = BANK // P

        @block.tensor
        def _(pe):
            pe.wait_ge(normed, 1)
            for j in range(JOBS):
                pair, first = divmod(j * PER, S.T)
                for k in range(PER):
                    last = nc.tensor.transpose(ps[:, j * BANK + k * P:j * BANK + (k + 1) * P],
                                               sb["h"][:, first + k, 2 * pair:2 * pair + 2, :]
                                               .rearrange("p b c -> p (b c)"), sb["ident"][:])
                last.then_inc(turned, 1)

        @block.scalar
        def _(act):
            for j in range(1, JOBS, 2):
                act.wait_ge(turned, j + 1)
                nc.scalar.copy(keys[0][:, j * BANK:(j + 1) * BANK], ps[:, j * BANK:(j + 1) * BANK]).then_inc(copied_a, 1)

        @block.vector
        def _(v):
            layer_norm_relu(nc, sb["x1"][:].rearrange("p t b c -> p (t b) c"), sb["h"][:].rearrange("p t b c -> p (t b) c"),
                            tmp[:], mean[:], var[:], y[:], t[:]).then_inc(normed, 1)
            for j in range(0, JOBS, 2):
                v.wait_ge(turned, j + 1)
                nc.vector.tensor_copy(keys[0][:, j * BANK:(j + 1) * BANK], ps[:, j * BANK:(j + 1) * BANK])
            v.wait_ge(copied_a, JOBS // 2)
            v.drain()
            src, dst = keys
            size = 2
            while size <= S.N:
                a, o = (x[:].rearrange("p (n k) -> p n k", k=size) for x in (src, dst))
                half = size // 2
                lo, hi = a[:, :, 0:half], a[:, :, size - 1:half - 1:-1]
                nc.vector.tensor_tensor(o[:, :, 0:half], lo, hi, ALU.min)
                nc.vector.tensor_tensor(o[:, :, size - 1:half - 1:-1], lo, hi, ALU.max)
                v.drain()
                src, dst = dst, src
                step = size // 4
                while step:
                    a, o = (x[:].rearrange("p (n two k) -> p n two k", two=2, k=step) for x in (src, dst))
                    nc.vector.tensor_tensor(o[:, :, 0, :], a[:, :, 0, :], a[:, :, 1, :], ALU.min)
                    nc.vector.tensor_tensor(o[:, :, 1, :], a[:, :, 0, :], a[:, :, 1, :], ALU.max)
                    v.drain()
                    src, dst = dst, src
                    step //= 2
                size *= 2
            nc.vector.tensor_copy(dst[:], src[:]).then_inc(is_sorted, 1)

        @block.sync
        def _(sp):
            sp.wait_ge(is_sorted, 1)
            for pair in range(BP):
                sp.dma_start(d["sorted"][2 * pair:2 * pair + 2].rearrange("b c n -> (b c) n"),
                             keys[(STEPS + 1) % 2][:, pair * S.N:(pair + 1) * S.N]).then_inc(stored, 16)
            sp.wait_ge(stored, 16 * BP)


def graph_phase(nc, S, d, sb):
    with ExitStack() as ctx:
        buf = lambda n, s, dt=FP32: ctx.enter_context(nc.sbuf_tensor(n, s, dt))
        sem = lambda n: ctx.enter_context(nc.semaphore(n))
        Q = len(TAUS)
        adj_t = [buf(f"cadj{u}", [P, S.N]) for u in range(2)]
        keep = buf("keep", [P, S.T, S.N], BF16)
        rem = buf("rem", [P, S.T, S.N], BF16)
        rank = buf("rank", [P, S.T, S.N], FP16)
        nearT = buf("nearT", [P, S.T, S.N], BF16)
        deg, odd, skip, first, second = (buf(n, [P, S.T]) for n in ("deg", "odd", "skip", "first", "second"))
        deg_i = buf("deg_i", [P, S.T], INT32)
        bias = buf("bias", [P, S.T, Q])
        level = [buf(f"level{w}", [P, S.N]) for w in range(2)]
        gap = [buf(f"gap{w}", [P, S.N]) for w in range(2)]
        below = [buf(f"below{w}", [P, S.T, S.N], BF16) for w in range(2)]
        own = [buf(f"own{w}", [P, S.T]) for w in range(2)]
        ramp = [buf(f"ramp{w}", [P, Q, S.N], BF16) for w in range(2)]
        agg = buf("agg", [P, S.T, Q, S.C])
        mix = buf("mix", [P, S.T, S.C])
        mixT = buf("mixT", [S.C, S.N])
        hidT = buf("hidT", [S.HID, S.N])
        res = buf("res", [P, S.T, S.C])
        ps = ctx.enter_context(nc.psum_tensor("ps_graph", [P, 8 * BANK], FP32))
        bank = lambda k, n=1: ps[:, k * BANK:(k + n) * BANK]

        adj_ready = [sem(f"cadj_ready{u}") for u in range(2)]
        level_ready = [sem(f"level_ready{w}") for w in range(2)]
        adj_read, near_made, turned, turn_read, near_done, deg_done = (
            sem(n) for n in ("cadj_read", "near_made", "c_turned", "turn_read", "near_done", "deg_done"))
        bias_done, own_copied, below_done = (
            sem(n) for n in ("bias_done", "own_copied", "below_done"))
        counted, ramped, summed, passed = sem("counted"), sem("ramped"), sem("summed"), sem("cpassed")
        mix_done, mixT_done, mixT_read, hid_done, hid_read, y_done, res_done, out_stored = (
            sem(n) for n in ("mix_done", "mixT_done", "mixT_read", "hid_done", "hid_read", "cy_done", "res_done", "out_stored"))
        block = ctx.enter_context(nc.Block())
        CB = 4
        HALVES = S.N // BANK
        CT = S.C * S.T

        @block.sync
        def _(sp):
            sp.sem_inc(out_stored, 16)
            with sp.Fori(0, S.B) as b:
                for k in range(S.T):
                    sp.wait_ge(adj_read, b * S.T + k + 1)
                    sp.dma_start(adj_t[k % 2][:], d["adj"][bass.ds(b, 1), k * P:(k + 1) * P, :]
                                 .rearrange("o p n -> (o p) n")).then_inc(adj_ready[k % 2], 16)
                with sp.Fori(0, S.C // 2) as c2:
                    for w in range(2):
                        c = b * S.C + c2 * 2 + w
                        sp.wait_ge(below_done, c + 1)
                        sp.dma_start(level[w][:], d["sorted"][bass.ds(b, 1), bass.ds(c2 * 2 + w, 1), :]
                                     .rearrange("o c n -> (o c) n").to_broadcast([P, S.N])).then_inc(level_ready[w], 16)
                sp.wait_ge(res_done, b + 1)
                sp.dma_start(d["out"][bass.ds(b, 1)].rearrange("o (t p) c -> p (o t) c", p=P),
                             res[:]).then_inc(out_stored, 16)
            sp.wait_ge(out_stored, 16 * S.B + 16)

        @block.gpsimd
        def _(pool):
            pool.sem_inc(below_done, 2)
            with pool.Fori(0, S.B) as b:
                with pool.Fori(0, S.C // 2) as c2:
                    for w in range(2):
                        c = b * S.C + c2 * 2 + w
                        pool.wait_ge(counted, (c + 1) * S.T)
                        nc.gpsimd.tensor_copy(own[w][:], sb["h"][:, :, bass.ds(b, 1), bass.ds(c2 * 2 + w, 1)]
                                              .rearrange("p t o c -> p (t o c)")).then_inc(own_copied, 1)
                        pool.wait_ge(summed, (c + 1) * S.T)
                        pool.wait_ge(own_copied, c + 1)
                        wait_alone(pool, level_ready[w], (b * (S.C // 2) + c2) * 16 + 16, passed)
                        for k in range(S.T):
                            nc.gpsimd.tensor_scalar(below[w][:, k, :], level[w][:], own[w][:, k:k + 1], None,
                                                    ALU.is_gt)
                        nc.gpsimd.tensor_tensor(gap[w][:, 1:], level[w][:, 1:], level[w][:, :-1], ALU.subtract)
                        nc.gpsimd.tensor_copy(gap[w][:, 0:1], level[w][:, 0:1])
                        pool.drain().then_inc(below_done, 1)

        @block.tensor
        def _(pe):
            pe.sem_inc(counted, 2 * S.T)
            with pe.Fori(0, S.B) as b:
                pe.wait_ge(near_made, b + 1)
                for k in range(S.T):
                    pe.wait_ge(turn_read, b * S.T + k + 1)
                    half = bank(k % 2).bitcast(BF16)
                    for i in range(S.T):
                        last = nc.tensor.transpose(half[:, i * P:(i + 1) * P], keep[:, i, k * P:(k + 1) * P], sb["ident_b"][:])
                    last.then_inc(turned, 1)
                pe.wait_ge(near_done, b + 1)
                for i in range(S.T):
                    for k in range(S.T):
                        last = nc.tensor.matmul(bank(2)[:, i:i + 1], nearT[:, k, i * P:(i + 1) * P], sb["ones_b"][:],
                                                start=(k == 0), stop=(k == S.T - 1))
                last.then_inc(deg_done, 1)
                with pe.Fori(0, S.C // 2) as c2:
                    pe.wait_ge(bias_done, b + 1)
                    for w in range(2):
                        c = b * S.C + c2 * 2 + w
                        pe.wait_ge(below_done, c + 3)
                        for i in range(S.T):
                            pe.wait_ge(ramped, c * S.T + i + 1)
                            for half in range(HALVES):
                                for k in range(S.T):
                                    last = nc.tensor.matmul(bank(2 * (i % CB) + half), nearT[:, k, i * P:(i + 1) * P],
                                                            below[w][:, k, half * BANK:(half + 1) * BANK],
                                                            start=(k == 0), stop=(k == S.T - 1))
                            last.then_inc(counted, 1)
                wait_alone(pe, mix_done, b + 1, passed)
                for k in range(S.T):
                    last = nc.tensor.transpose(ps[0:S.C, k * P:(k + 1) * P], mix[:, k, :], sb["ident"][:])
                last.then_inc(mixT_done, 1)
                pe.wait_ge(mixT_read, b + 1)
                for half in range(HALVES):
                    last = nc.tensor.matmul(bank(2 + half)[0:S.HID, :], sb["w1"][:], mixT[:, half * BANK:(half + 1) * BANK],
                                            start=True, stop=True)
                last.then_inc(hid_done, 1)
                pe.wait_ge(hid_read, b + 1)
                for k in range(S.T):
                    last = nc.tensor.matmul(bank(4)[:, k * S.C:(k + 1) * S.C], hidT[:, k * P:(k + 1) * P], sb["w2"][:],
                                            start=True, stop=True)
                last.then_inc(y_done, 1)

        @block.scalar
        def _(act):
            act.sem_inc(ramped, CB)
            with act.Fori(0, S.B) as b:
                with act.Fori(0, S.C // 2) as c2:
                    act.wait_ge(bias_done, b + 1)
                    for w in range(2):
                        for i in range(S.T):
                            g = (b * S.C + c2 * 2 + w) * S.T + i
                            act.wait_ge(counted, g + 1 + 2 * S.T)
                            act.wait_ge(summed, g + S.T * 2 - 1)
                            for q in range(Q):
                                last = nc.scalar.activation(ramp[i % 2][:, q, :], bank(2 * (i % CB), 2), ACT.Relu,
                                                            bias=bias[:, i, q:q + 1], scale=-WTS[q])
                            last.then_inc(ramped, 1)
                act.wait_ge(hid_done, b + 1)
                nc.scalar.activation(hidT[:], bank(2, 2)[0:S.HID, :], ACT.Relu, bias=sb["b1"][:]).then_inc(hid_read, 1)

        @block.vector
        def _(v):
            v.sem_inc(adj_read, 2)
            v.sem_inc(turn_read, 2)
            v.sem_inc(summed, 2 * S.T)
            with v.Fori(0, S.B) as b:
                for k in range(S.T):
                    v.wait_ge(adj_ready[k % 2], (b * (S.T // 2) + k // 2) * 16 + 16)
                    nc.vector.tensor_scalar(keep[:, k, :], adj_t[k % 2][:], 0.0, None, ALU.is_gt).then_inc(adj_read, 1)
                    v.drain()
                    own_block = keep[:, k, k * P:(k + 1) * P]
                    nc.vector.tensor_tensor(own_block, own_block, sb["off_diag"][:], ALU.mult)
                    v.drain()
                    nc.vector.tensor_tensor_scan(rank[:, k, :], keep[:, k, :], keep[:, k, :], 0.0, ALU.add, ALU.max)
                v.drain()
                nc.vector.tensor_copy(deg[:], rank[:, :, S.N - 1])
                v.drain()
                nc.vector.tensor_copy(deg_i[:], deg[:])
                v.drain()
                nc.vector.tensor_scalar(deg_i[:], deg_i[:], 1, None, ALU.bitwise_and)
                v.drain()
                nc.vector.tensor_copy(odd[:], deg_i[:])
                v.drain()
                nc.vector.tensor_tensor(skip[:], deg[:], odd[:], ALU.add)
                v.drain()
                nc.vector.tensor_scalar(odd[:], deg[:], DEG_T, None, ALU.is_gt)
                v.drain()
                nc.vector.tensor_tensor(odd[:], odd[:], sb["mask"][:, bass.ds(b * S.T, S.T)], ALU.mult)
                v.drain()
                nc.vector.tensor_tensor(second[:], skip[:], odd[:], ALU.mult)
                v.drain()
                nc.vector.tensor_scalar(first[:], second[:], 0.5, None, ALU.mult)
                v.drain()
                for k in range(S.T):
                    nc.vector.tensor_scalar(rem[:, k, :], rank[:, k, :], first[:, k:k + 1], None, ALU.is_equal)
                v.drain()
                for k in range(S.T):
                    nc.vector.scalar_tensor_tensor(rem[:, k, :], rank[:, k, :], second[:, k:k + 1], rem[:, k, :],
                                                   ALU.is_equal, ALU.add)
                v.drain()
                nc.vector.tensor_tensor(rem[:], rem[:], keep[:], ALU.mult)
                v.drain()
                nc.vector.tensor_tensor(keep[:], keep[:], rem[:], ALU.subtract).then_inc(near_made, 1)
                for k in range(S.T):
                    v.wait_ge(turned, b * S.T + k + 1)
                    nc.vector.scalar_tensor_tensor(nearT[:, k, :], rem[:, k, :], 0.0, bank(k % 2).bitcast(BF16),
                                                   ALU.is_equal, ALU.mult).then_inc(turn_read, 1)
                    v.drain()
                    own_block = nearT[:, k, k * P:(k + 1) * P]
                    last = nc.vector.tensor_tensor(own_block, own_block, sb["ident_b"][:], ALU.max)
                last.then_inc(near_done, 1)
                v.wait_ge(deg_done, b + 1)
                for q in range(Q):
                    last = nc.vector.tensor_scalar(bias[:, :, q], bank(2)[:, 0:S.T], WTS[q] * TAUS[q],
                                                   WTS[q] * (1.0 - TAUS[q]), ALU.mult, ALU.add)
                last.then_inc(bias_done, 1)
                with v.Fori(0, S.C // 2) as c2:
                    for w in range(2):
                        for i in range(S.T):
                            g = (b * S.C + c2 * 2 + w) * S.T + i
                            v.wait_ge(ramped, g + 1 + CB)
                            for q in range(Q):
                                last = nc.vector.scalar_tensor_tensor(
                                    ramp[i % 2][:, q, :], ramp[i % 2][:, q, :], WTS[q], gap[w][:], ALU.min, ALU.mult,
                                    accum_out=agg[:, i, q, bass.ds(c2 * 2 + w, 1)])
                            last.then_inc(summed, 1)
                v.drain()
                nc.vector.tensor_tensor(mix[:], agg[:, :, 0, :], agg[:, :, 1, :], ALU.add)
                v.drain()
                nc.vector.tensor_tensor(mix[:], mix[:], agg[:, :, 2, :], ALU.add)
                v.drain()
                nc.vector.tensor_tensor(mix[:], mix[:], sb["h"][:, :, bass.ds(b, 1), :].rearrange("p t o c -> p (t o) c"),
                                        ALU.add).then_inc(mix_done, 1)
                v.wait_ge(mixT_done, b + 1)
                nc.vector.tensor_copy(mixT[:], ps[0:S.C, 0:S.N]).then_inc(mixT_read, 1)
                v.wait_ge(y_done, b + 1)
                v.wait_ge(out_stored, b * 16 + 16)
                nc.vector.tensor_tensor(res[:], bank(4)[:, 0:S.T * S.C].rearrange("p (t c) -> p t c", c=S.C),
                                        sb["b2"][:][:, None, :].to_broadcast([P, S.T, S.C]), ALU.add)
                v.drain()
                nc.vector.tensor_tensor(res[:], res[:], sb["mask"][:, bass.ds(b * S.T, S.T)][:, :, None]
                                        .to_broadcast([P, S.T, S.C]), ALU.mult)
                v.drain()
                nc.vector.tensor_tensor(res[:], res[:], sb["x1"][:, :, bass.ds(b, 1), :].rearrange("p t o c -> p (t o) c"),
                                        ALU.add).then_inc(res_done, 1)


def build(nc, x, adj, mask, w_qkv, w_proj, b_proj, w_gamma, b_gamma, w1, b1, w2, b2, out):
    S = Shapes(x, w_qkv, w1)
    d = dict(x=x, adj=adj, mask=mask, w_qkv=w_qkv, w_proj=w_proj, b_proj=b_proj, w_gamma=w_gamma,
             b_gamma=b_gamma, w1=w1, b1=b1, w2=w2, b2=b2, out=out)
    d["sorted"] = nc.dram_tensor("sorted_levels", [S.B, S.C, S.N], FP32).ap()
    with ExitStack() as ctx:
        sb = {}
        for name, shape, dt in (
            ("x1", [P, S.T, S.B, S.C], FP32),
            ("h", [P, S.T, S.B, S.C], FP32),
            ("ident", [P, P], FP32), ("ones", [P, P], FP32), ("off_diag", [P, P], FP32),
            ("ident_b", [P, P], BF16), ("ones_b", [P, 1], BF16),
            ("wqkvT", [S.C, 3 * S.F], FP32), ("wprojT", [P, S.F // P, S.C], FP32),
            ("wgam", [S.C, 2], FP32), ("wgam0", [S.C, P], FP32), ("bgam", [P, 2], FP32), ("bproj", [P, S.C], FP32),
            ("w1", [S.C, S.HID], FP32), ("b1", [S.HID, 1], FP32), ("w2", [S.HID, S.C], FP32), ("b2", [P, S.C], FP32),
            ("mask", [P, S.B * S.T], FP32),
        ):
            sb[name] = ctx.enter_context(nc.sbuf_tensor("k_" + name, shape, dt))
        setup_phase(nc, S, d, sb)
        attention_phase(nc, S, d, sb)
        sort_phase(nc, S, d, sb)
        graph_phase(nc, S, d, sb)


_INS = ["x", "adj", "nodemask", "L0_gnn_W_qkv", "L0_gnn_W_proj", "L0_gnn_b_proj", "L0_gnn_W_gamma", "L0_gnn_b_gamma",
        "L1_gnn_W1", "L1_gnn_b1", "L1_gnn_W2", "L1_gnn_b2"]


def kernel(**inputs):
    import numpy as np
    import concourse.bacc as bacc
    from concourse.bass_utils import run_bass_kernel_spmd

    nc = bacc.Bacc("TRN2", target_bir_lowering=False, num_devices=1)
    arrays, args = {}, []
    for name in _INS:
        a = np.ascontiguousarray(inputs[name])
        if a.dtype == np.bool_:
            a = a.view(np.uint8)
        arrays[f"in_{name}"] = a
        args.append(nc.dram_tensor(f"in_{name}", a.shape, mybir.dt.from_np(a.dtype), kind="ExternalInput").ap())
    shape = tuple(np.shape(inputs["x"]))
    out = nc.dram_tensor("out_x", shape, FP32, kind="ExternalOutput").ap()
    build(nc, *args, out)
    r = run_bass_kernel_spmd(nc, [arrays], core_ids=[0])
    return r.results[0]["out_x"]
```

```python
import concourse.bass as bass
from concourse import mybir
from contextlib import ExitStack

FP32 = mybir.dt.float32
BF16 = mybir.dt.bfloat16
FP16 = mybir.dt.float16
INT32 = mybir.dt.int32
UINT8 = mybir.dt.uint8
ALU = mybir.AluOpType
ACT = mybir.ActivationFunctionType
AX = mybir.AxisListType

P = 128
BANK = 512


class Shapes:

    def __init__(self, x, w_qkv, w1):
        self.B, self.N, self.C = x.shape
        self.T = self.N // P
        self.F = w_qkv.shape[0] // 3
        self.D = self.C
        self.H = self.F // self.D
        self.HP = self.H // 2
        self.HID = w1.shape[1]


TAUS = (0.25, 0.5, 0.75)
WTS = (0.25, 0.5, 0.25)
DEG_T = 10.0
EPS = 1e-5


def wait_alone(eng, sem, value, passed):
    eng.wait_ge(sem, value)
    eng.sem_inc(passed, 1)


def layer_norm_relu(nc, x, h, tmp, mean, var, y, t):
    v = nc.vector
    G, C = x.shape[1], x.shape[2]
    v.reduce_sum(mean, x, axis=AX.X)
    v.drain()
    v.tensor_scalar(mean, mean, 1.0 / C, None, ALU.mult)
    v.drain()
    v.tensor_tensor(h, x, mean[:, :, None].to_broadcast([P, G, C]), ALU.subtract)
    v.drain()
    v.tensor_tensor(tmp, h, h, ALU.mult)
    v.drain()
    v.reduce_sum(var, tmp, axis=AX.X)
    v.drain()
    v.tensor_scalar(var, var, 1.0 / C, EPS, ALU.mult, ALU.add)
    v.drain()
    v.tensor_scalar(t.bitcast(INT32), var.bitcast(INT32), 1, None, ALU.logical_shift_right)
    v.drain()
    v.tensor_scalar(y.bitcast(INT32), t.bitcast(INT32), -1.0, 1597463007.0, ALU.mult, ALU.add)
    v.drain()
    for _ in range(4):
        v.tensor_tensor(t, y, y, ALU.mult)
        v.drain()
        v.tensor_tensor(t, t, var, ALU.mult)
        v.drain()
        v.tensor_scalar(t, t, -0.5, 1.5, ALU.mult, ALU.add)
        v.drain()
        v.tensor_tensor(y, y, t, ALU.mult)
        v.drain()
    v.tensor_tensor(tmp, h, y[:, :, None].to_broadcast([P, G, C]), ALU.mult)
    v.drain()
    return v.tensor_scalar(h, tmp, 0.0, None, ALU.max)


def setup_phase(nc, S, d, sb):
    with ExitStack() as ctx:
        buf = lambda n, s, dt=FP32: ctx.enter_context(nc.sbuf_tensor(n, s, dt))
        sem = lambda n: ctx.enter_context(nc.semaphore(n))
        KT = 3 * S.F // P
        wqkv_rows = buf("wqkv_rows", [P, KT, S.C])
        wproj_rows = buf("wproj_rows", [S.C, S.F])
        wgam_rows = buf("wgam_rows", [2, S.C])
        mask_rows = buf("mask_rows", [S.B * S.T, P], UINT8)
        mask_rows_f = buf("mask_rows_f", [S.B * S.T, P])
        upto = buf("upto", [P, P])
        slot_i = buf("slot_i", [P, max(SLOTS)], INT32)
        tmp = buf("ln_tmp0", [P, S.T * S.B, S.C])
        mean, var, y, t = (buf(f"ln0_{n}", [P, S.T * S.B]) for n in ("mean", "var", "y", "t"))
        ps = ctx.enter_context(nc.psum_tensor("ps_setup", [P, 8 * BANK], FP32))
        loaded_x, loaded_w, ident_done, ones_done = sem("su_x"), sem("su_w"), sem("su_id"), sem("su_one")
        copied, turned = sem("su_copied"), sem("su_turned")
        block = ctx.enter_context(nc.Block())

        @block.sync
        def _(sp):
            for b in range(S.B):
                sp.dma_start(sb["x1"][:, :, b, :], d["x"][b].rearrange("(t p) c -> p t c", p=P)).then_inc(loaded_x, 16)

        @block.scalar
        def _(act):
            for dst, src in (
                (wqkv_rows[:], d["w_qkv"].rearrange("(t p) c -> p t c", p=P)),
                (wproj_rows[:], d["w_proj"]),
                (wgam_rows[:], d["w_gamma"]),
                (mask_rows[:], d["mask"].rearrange("b (t p) -> (b t) p", p=P)),
                (sb["bproj"][:], d["b_proj"][None, :].to_broadcast([P, S.C])),
                (sb["bgam"][:], d["b_gamma"][None, :].to_broadcast([P, 2])),
                (sb["w1"][:], d["w1"]),
                (sb["b1"][:], d["b1"][:, None]),
                (sb["w2"][:], d["w2"]),
                (sb["b2"][:], d["b2"][None, :].to_broadcast([P, S.C])),
            ):
                act.dma_start(dst, src).then_inc(loaded_w, 16)

        @block.gpsimd
        def _(pool):
            nc.gpsimd.memset(sb["ident"][:], 0.0)
            nc.gpsimd.memset(sb["ones"][:], 1.0).then_inc(ones_done, 1)
            pool.wait_ge(ones_done, 1)
            nc.gpsimd.affine_select(out=sb["ident"][:], in_=sb["ident"][:], compare_op=ALU.not_equal, fill=1.0,
                                    base=0, pattern=[[-1, P]], channel_multiplier=1)
            nc.gpsimd.affine_select(out=upto[:], in_=sb["ones"][:], compare_op=ALU.is_ge, fill=0.0,
                                    base=0, pattern=[[1, P]], channel_multiplier=-1)
            nc.gpsimd.iota(slot_i[:], pattern=[[1, max(SLOTS)]], base=0, channel_multiplier=0)
            pool.drain().then_inc(ident_done, 1)

        @block.tensor
        def _(pe):
            pe.wait_ge(loaded_w, 160)
            pe.wait_ge(ident_done, 1)
            for k in range(KT):
                nc.tensor.transpose(ps[0:S.C, k * P:(k + 1) * P], wqkv_rows[:, k, :], sb["ident"][:])
            for k in range(S.F // P):
                nc.tensor.transpose(ps[:, 3 * BANK + k * S.C:3 * BANK + (k + 1) * S.C],
                                    wproj_rows[:, k * P:(k + 1) * P], sb["ident"][0:S.C, 0:S.C])
            nc.tensor.transpose(ps[0:S.C, 5 * BANK:5 * BANK + 2], wgam_rows[:], sb["ident"][0:2, 0:2])
            pe.wait_ge(copied, 1)
            nc.tensor.transpose(ps[:, 4 * BANK:4 * BANK + S.B * S.T], mask_rows_f[:],
                                sb["ident"][0:S.B * S.T, 0:S.B * S.T]).then_inc(turned, 1)

        @block.vector
        def _(v):
            v.wait_ge(loaded_w, 160)
            nc.vector.tensor_copy(mask_rows_f[:], mask_rows[:]).then_inc(copied, 1)
            v.wait_ge(ident_done, 1)
            nc.vector.tensor_copy(sb["ident_b"][:], sb["ident"][:])
            nc.vector.tensor_copy(sb["ones_b"][:], sb["ones"][:])
            nc.vector.tensor_copy(sb["upto_b"][:], upto[:])
            nc.vector.tensor_copy(sb["slot"][:], slot_i[:])
            nc.vector.tensor_scalar(sb["off_diag"][:], sb["ident"][:], -1.0, 1.0, ALU.mult, ALU.add)
            v.wait_ge(loaded_x, 16 * S.B)
            layer_norm_relu(nc, sb["x1"][:].rearrange("p t b c -> p (t b) c"), sb["h"][:].rearrange("p t b c -> p (t b) c"),
                            tmp[:], mean[:], var[:], y[:], t[:])
            v.wait_ge(turned, 1)
            nc.vector.tensor_scalar(sb["wqkvT"][:, 0:S.F], ps[0:S.C, 0:S.F], S.D ** -0.5, None, ALU.mult)
            nc.vector.tensor_copy(sb["wqkvT"][:, S.F:], ps[0:S.C, S.F:3 * S.F])
            nc.vector.tensor_copy(sb["wprojT"][:].rearrange("p k c -> p (k c)"),
                                  ps[:, 3 * BANK:3 * BANK + S.F // P * S.C])
            nc.vector.tensor_copy(sb["wgam"][:], ps[0:S.C, 5 * BANK:5 * BANK + 2])
            nc.vector.tensor_copy(sb["wgam0"][:], ps[0:S.C, 5 * BANK:5 * BANK + 1].to_broadcast([S.C, P]))
            nc.vector.tensor_copy(sb["mask"][:], ps[:, 4 * BANK:4 * BANK + S.B * S.T])


def attention_phase(nc, S, d, sb):
    with ExitStack() as ctx:
        buf = lambda n, s, dt=FP32: ctx.enter_context(nc.sbuf_tensor(n, s, dt))
        sem = lambda n: ctx.enter_context(nc.semaphore(n))
        h_b = buf("h_b", [P, S.T, S.C])
        hT = buf("hT", [S.C, S.N])
        g0 = buf("g0", [P, S.N])
        g1 = buf("g1", [P, S.T])
        kT = buf("kT", [P, S.HP, S.N])
        vals = buf("vals", [P, S.T, S.F])
        adj_t = [buf(f"adj_t{u}", [P, S.N]) for u in range(2)]
        bias_t = [buf(f"bias_t{u}", [P, S.N]) for u in range(2)]
        qT = [buf(f"qT{u}", [P, S.HP, P]) for u in range(2)]
        neg = [buf(f"neg{u}", [P, S.N]) for u in range(2)]
        prob = [buf(f"prob{u}", [P, S.N]) for u in range(2)]
        probT = [buf(f"probT{u}", [P, S.T, P]) for u in range(2)]
        neg_max = [buf(f"neg_max{u}", [P, S.H]) for u in range(2)]
        row_sum = [buf(f"row_sum{u}", [P, S.H]) for u in range(2)]
        row_inv = buf("row_inv", [P, S.H])
        o_sb = buf("o_sb", [P, S.F])
        oT = buf("oT", [P, S.F // P, P])
        y_sb = buf("y_sb", [P, S.C])
        ps = ctx.enter_context(nc.psum_tensor("ps_att", [P, 8 * BANK], FP32))
        bank = lambda k, n=1: ps[:, k * BANK:(k + n) * BANK]
        PT0, OB, MB = 4, 6, 7

        adj_ready = [sem(f"adj_ready{u}") for u in range(2)]
        adj_free = sem("adj_free")
        h_ready, passed = sem("h_ready"), sem("passed")
        job_done, job_read_v, job_read_a = sem("job_done"), sem("job_read_v"), sem("job_read_a")
        q_done, q_read = sem("q_done"), sem("q_read")
        s_done, s_read = sem("s_done"), sem("s_read")
        p_done = sem("p_done")
        t_done, t_read_v, t_read_a = sem("t_done"), sem("t_read_v"), sem("t_read_a")
        pv_done, o_norm, oT_done, oT_read = sem("pv_done"), sem("o_norm"), sem("oT_done"), sem("oT_read")
        y_done, tile_done = sem("y_done"), sem("tile_done")
        block = ctx.enter_context(nc.Block())

        HALVES = S.N // BANK
        K0 = 5
        V0 = K0 + S.HP * HALVES
        JOBS = V0 + S.T
        by_act = lambda j: j in (2, 3, 4) or (j >= K0 and j % 2 == 0)
        n_act = lambda j: sum(by_act(i) for i in range(j + 1))
        n_vec = lambda j: j + 1 - n_act(j)
        JA, JV = n_act(JOBS - 1), n_vec(JOBS - 1)

        @block.sync
        def _(sp):
            with sp.Fori(0, S.B) as b:
                with sp.Fori(0, S.T // 2) as i2:
                    for u in range(2):
                        n = b * S.T + i2 * 2 + u
                        sp.wait_ge(adj_free, n + 1)
                        sp.dma_start(adj_t[u][:], d["adj"][bass.ds(b, 1), bass.ds(i2 * (2 * P) + u * P, P), :]
                                     .rearrange("o p n -> (o p) n")).then_inc(adj_ready[u], 16)

        @block.tensor
        def _(pe):
            with pe.Fori(0, S.B) as b:
                wait_alone(pe, h_ready, b + 1, passed)
                for j in range(JOBS):
                    if j >= 8:
                        if by_act(j - 8):
                            pe.wait_ge(job_read_a, b * JA + n_act(j - 8))
                        else:
                            pe.wait_ge(job_read_v, b * JV + n_vec(j - 8))
                    if j < 2:
                        for k in range(BANK // P):
                            last = nc.tensor.transpose(bank(j)[0:S.C, k * P:(k + 1) * P],
                                                       h_b[:, j * (BANK // P) + k, :], sb["ident"][:])
                        last.then_inc(job_done, 1)
                        if j == 1:
                            pe.wait_ge(job_read_v, b * JV + 2)
                    elif j < 4:
                        nc.tensor.matmul(bank(j), sb["wgam0"][:], hT[:, (j - 2) * BANK:(j - 1) * BANK],
                                         start=True, stop=True).then_inc(job_done, 1)
                    elif j == 4:
                        for k in range(S.T):
                            last = nc.tensor.matmul(bank(j)[:, 2 * k:2 * k + 2], hT[:, k * P:(k + 1) * P],
                                                    sb["wgam"][:], start=True, stop=True)
                        last.then_inc(job_done, 1)
                    elif j < V0:
                        pair, half = divmod(j - K0, HALVES)
                        nc.tensor.matmul(bank(j % 8), sb["wqkvT"][:, S.F + pair * P:S.F + (pair + 1) * P],
                                         hT[:, half * BANK:(half + 1) * BANK],
                                         start=True, stop=True).then_inc(job_done, 1)
                    else:
                        k = j - V0
                        nc.tensor.matmul(bank(j % 8), hT[:, k * P:(k + 1) * P], sb["wqkvT"][:, 2 * S.F:3 * S.F],
                                         start=True, stop=True).then_inc(job_done, 1)
                with pe.Fori(0, S.T // 2) as i2:
                    pe.wait_ge(job_read_a, b * JA + JA)
                    pe.wait_ge(job_read_v, b * JV + JV)
                    for u in range(2):
                        n = b * S.T + i2 * 2 + u
                        pe.wait_ge(tile_done, n + 1)
                        for pair in range(S.HP):
                            last = nc.tensor.matmul(bank(MB)[:, pair * P:(pair + 1) * P],
                                                    sb["wqkvT"][:, pair * P:(pair + 1) * P],
                                                    hT[:, bass.ds(i2 * (2 * P) + u * P, P)], start=True, stop=True)
                        last.then_inc(q_done, 1)

                        def scores(h):
                            g = n * S.H + h
                            pe.wait_ge(s_read, g + 1)
                            r = (h % 2) * S.D
                            for half in range(HALVES):
                                last = nc.tensor.matmul(ps[:, (2 * (h % 2) + half) * BANK:(2 * (h % 2) + half + 1) * BANK],
                                                        qT[u][r:r + S.D, h // 2, :],
                                                        kT[r:r + S.D, h // 2, half * BANK:(half + 1) * BANK],
                                                        start=True, stop=True)
                            last.then_inc(s_done, 1)

                        def turn(h):
                            g = n * S.H + h
                            pe.wait_ge(p_done, g + 3)
                            for half in range(HALVES):
                                pe.wait_ge(t_read_a if half else t_read_v, g + 1)
                                for k in range(BANK // P):
                                    c = half * BANK + k * P
                                    last = nc.tensor.transpose(bank(PT0 + half)[:, k * P:(k + 1) * P],
                                                               prob[h % 2][:, c:c + P], sb["ident"][:])
                                last.then_inc(t_done, 1)

                        def weigh(h):
                            g = n * S.H + h
                            pe.wait_ge(t_read_a, g + 2)
                            pe.wait_ge(t_read_v, g + 2)
                            for k in range(S.T):
                                last = nc.tensor.matmul(bank(OB)[:, h * S.D:(h + 1) * S.D], probT[h % 2][:, k, :],
                                                        vals[:, k, h * S.D:(h + 1) * S.D],
                                                        start=(k == 0), stop=(k == S.T - 1))
                            last.then_inc(pv_done, 1)

                        pe.wait_ge(q_read, n + 1)
                        scores(0)
                        for h in range(S.H):
                            if h + 1 < S.H:
                                scores(h + 1)
                            turn(h)
                            if h:
                                weigh(h - 1)
                        weigh(S.H - 1)
                        pe.wait_ge(o_norm, n + 1)
                        for k in range(S.F // P):
                            last = nc.tensor.transpose(bank(MB)[:, k * P:(k + 1) * P], o_sb[:, k * P:(k + 1) * P],
                                                       sb["ident"][:])
                        last.then_inc(oT_done, 1)
                        pe.wait_ge(oT_read, n + 1)
                        for k in range(S.F // P):
                            last = nc.tensor.matmul(bank(MB)[:, 0:S.C], oT[:, k, :], sb["wprojT"][:, k, :],
                                                    start=(k == 0), stop=(k == S.F // P - 1))
                        last.then_inc(y_done, 1)

        @block.scalar
        def _(act):
            act.sem_inc(t_read_a, 1)
            act.sem_inc(p_done, 2)
            with act.Fori(0, S.B) as b:
                for j in range(JOBS):
                    if not by_act(j):
                        continue
                    act.wait_ge(job_done, b * JOBS + j + 1)
                    if j < 4:
                        i = nc.scalar.activation(g0[:, (j - 2) * BANK:(j - 1) * BANK], bank(j), ACT.Exp,
                                                 bias=sb["bgam"][:, 0:1])
                    elif j == 4:
                        i = nc.scalar.activation(g1[:], bank(j)[:, 1:2 * S.T:2], ACT.Exp, bias=sb["bgam"][:, 1:2])
                    elif j < V0:
                        pair, half = divmod(j - K0, HALVES)
                        i = nc.scalar.copy(kT[:, pair, half * BANK:(half + 1) * BANK], bank(j % 8))
                    else:
                        i = nc.scalar.copy(vals[:, j - V0, :], bank(j % 8))
                    i.then_inc(job_read_a, 1)
                with act.Fori(0, S.T // 2) as i2:
                    for u in range(2):
                        n = b * S.T + i2 * 2 + u

                        def exps(h):
                            g = n * S.H + h
                            act.wait_ge(s_read, g + 3)
                            act.wait_ge(t_done, g * 2 + 1)
                            nc.scalar.activation(prob[h % 2][:], neg[h % 2][:], ACT.Exp, scale=-1.0,
                                                 bias=neg_max[u][:, h:h + 1],
                                                 accum_out=row_sum[u][:, h:h + 1]).then_inc(p_done, 1)

                        def evac(h):
                            g = n * S.H + h
                            act.wait_ge(t_done, g * 2 + 2 + 3)
                            act.wait_ge(pv_done, g + 1)
                            nc.scalar.copy(probT[h % 2][:, S.T // 2:, :].rearrange("p t q -> p (t q)"),
                                           bank(PT0 + 1)).then_inc(t_read_a, 1)

                        exps(0)
                        for h in range(S.H):
                            if h + 1 < S.H:
                                exps(h + 1)
                            evac(h)

        @block.vector
        def _(v):
            v.sem_inc(t_read_v, 1)
            v.sem_inc(s_read, 2)
            v.sem_inc(tile_done, 1)
            v.sem_inc(adj_free, 2)
            v.sem_inc(t_done, 3)
            v.sem_inc(pv_done, 2)
            with v.Fori(0, S.B) as b:
                nc.vector.tensor_copy(h_b[:], sb["h"][:, :, bass.ds(b, 1), :].rearrange("p t o c -> p (t o) c")).then_inc(h_ready, 1)
                for j in range(JOBS):
                    if by_act(j):
                        continue
                    v.wait_ge(job_done, b * JOBS + j + 1)
                    if j < 2:
                        i = nc.vector.tensor_copy(hT[:, j * BANK:(j + 1) * BANK], bank(j)[0:S.C, :])
                    elif j < V0:
                        pair, half = divmod(j - K0, HALVES)
                        i = nc.vector.tensor_copy(kT[:, pair, half * BANK:(half + 1) * BANK], bank(j % 8))
                    else:
                        i = nc.vector.tensor_copy(vals[:, j - V0, :], bank(j % 8))
                    i.then_inc(job_read_v, 1)
                with v.Fori(0, S.T // 2) as i2:
                    v.wait_ge(job_read_a, b * JA + JA)
                    for u in range(2):
                        n = b * S.T + i2 * 2 + u
                        v.wait_ge(adj_ready[u], (b * (S.T // 2) + i2) * 16 + 16)
                        nc.vector.tensor_scalar(bias_t[u][:], adj_t[u][:], g1[:, bass.ds(i2 * 2 + u, 1)], None,
                                                ALU.mult).then_inc(adj_free, 1)
                        v.wait_ge(q_done, n + 1)
                        nc.vector.tensor_tensor(
                            qT[u][:], bank(MB).rearrange("p (h q) -> p h q", q=P),
                            g0[:, bass.ds(i2 * (2 * P) + u * P, P)][:, None, :].to_broadcast([P, S.HP, P]),
                            ALU.mult).then_inc(q_read, 1)
                        v.drain()

                        def take_max(h):
                            g = n * S.H + h
                            v.wait_ge(s_done, g + 1)
                            wait_alone(v, p_done, g + 1, passed)
                            nc.vector.tensor_tensor_reduce(
                                out=neg[h % 2][:], in0=ps[:, 2 * (h % 2) * BANK:(2 * (h % 2) + 2) * BANK],
                                in1=bias_t[u][:], scale=-1.0, scalar=3.0e38, op0=ALU.add, op1=ALU.min,
                                accum_out=neg_max[u][:, h:h + 1]).then_inc(s_read, 1)

                        def evac(h):
                            g = n * S.H + h
                            v.wait_ge(t_done, g * 2 + 1 + 3)
                            v.wait_ge(pv_done, g + 1)
                            nc.vector.tensor_copy(probT[h % 2][:, 0:S.T // 2, :].rearrange("p t q -> p (t q)"),
                                                  bank(PT0)).then_inc(t_read_v, 1)

                        take_max(0)
                        for h in range(S.H):
                            if h + 1 < S.H:
                                take_max(h + 1)
                            evac(h)
                        v.wait_ge(pv_done, n * S.H + S.H + 2)
                        nc.vector.reciprocal(row_inv[:], row_sum[u][:])
                        v.drain()
                        nc.vector.tensor_tensor(o_sb[:].rearrange("p (h d) -> p h d", d=S.D),
                                                bank(OB).rearrange("p (h d) -> p h d", d=S.D),
                                                row_inv[:, :, None].to_broadcast([P, S.H, S.D]),
                                                ALU.mult).then_inc(o_norm, 1)
                        v.wait_ge(oT_done, n + 1)
                        nc.vector.tensor_copy(oT[:].rearrange("p k q -> p (k q)"), bank(MB)).then_inc(oT_read, 1)
                        v.wait_ge(y_done, n + 1)
                        nc.vector.tensor_tensor(y_sb[:], bank(MB)[:, 0:S.C], sb["bproj"][:], ALU.add)
                        v.drain()
                        x1 = sb["x1"][:, bass.ds(i2 * 2 + u, 1), bass.ds(b, 1), :].rearrange("p t b c -> p (t b c)")
                        nc.vector.tensor_tensor(x1, x1, y_sb[:], ALU.add).then_inc(tile_done, 1)


def sort_phase(nc, S, d, sb):
    with ExitStack() as ctx:
        buf = lambda n, s, dt=FP32: ctx.enter_context(nc.sbuf_tensor(n, s, dt))
        sem = lambda n: ctx.enter_context(nc.semaphore(n))
        BP = S.B // 2
        tmp = buf("ln_tmp1", [P, S.T * S.B, S.C])
        mean, var, y, t = (buf(f"ln1_{n}", [P, S.T * S.B]) for n in ("mean", "var", "y", "t"))
        keys = [buf(f"keys{i}", [P, BP * S.N]) for i in range(2)]
        ps = ctx.enter_context(nc.psum_tensor("ps_sort", [P, 8 * BANK], FP32))
        normed, turned, copied_v, copied_a, is_sorted, stored = (
            sem(n) for n in ("so_normed", "so_turned", "so_copied_v", "so_copied_a", "so_sorted", "so_stored"))
        block = ctx.enter_context(nc.Block())
        levels = S.N.bit_length() - 1
        STEPS = levels * (levels + 1) // 2
        JOBS = BP * S.N // BANK
        PER = BANK // P

        @block.tensor
        def _(pe):
            pe.wait_ge(normed, 1)
            for j in range(JOBS):
                pair, first = divmod(j * PER, S.T)
                for k in range(PER):
                    last = nc.tensor.transpose(ps[:, j * BANK + k * P:j * BANK + (k + 1) * P],
                                               sb["h"][:, first + k, 2 * pair:2 * pair + 2, :]
                                               .rearrange("p b c -> p (b c)"), sb["ident"][:])
                last.then_inc(turned, 1)

        @block.scalar
        def _(act):
            for j in range(1, JOBS, 2):
                act.wait_ge(turned, j + 1)
                nc.scalar.copy(keys[0][:, j * BANK:(j + 1) * BANK], ps[:, j * BANK:(j + 1) * BANK]).then_inc(copied_a, 1)

        @block.vector
        def _(v):
            layer_norm_relu(nc, sb["x1"][:].rearrange("p t b c -> p (t b) c"), sb["h"][:].rearrange("p t b c -> p (t b) c"),
                            tmp[:], mean[:], var[:], y[:], t[:]).then_inc(normed, 1)
            for j in range(0, JOBS, 2):
                v.wait_ge(turned, j + 1)
                nc.vector.tensor_copy(keys[0][:, j * BANK:(j + 1) * BANK], ps[:, j * BANK:(j + 1) * BANK])
            v.wait_ge(copied_a, JOBS // 2)
            v.drain()
            src, dst = keys
            size = 2
            while size <= S.N:
                a, o = (x[:].rearrange("p (n k) -> p n k", k=size) for x in (src, dst))
                half = size // 2
                lo, hi = a[:, :, 0:half], a[:, :, size - 1:half - 1:-1]
                nc.vector.tensor_tensor(o[:, :, 0:half], lo, hi, ALU.min)
                nc.vector.tensor_tensor(o[:, :, size - 1:half - 1:-1], lo, hi, ALU.max)
                v.drain()
                src, dst = dst, src
                step = size // 4
                while step:
                    a, o = (x[:].rearrange("p (n two k) -> p n two k", two=2, k=step) for x in (src, dst))
                    nc.vector.tensor_tensor(o[:, :, 0, :], a[:, :, 0, :], a[:, :, 1, :], ALU.min)
                    nc.vector.tensor_tensor(o[:, :, 1, :], a[:, :, 0, :], a[:, :, 1, :], ALU.max)
                    v.drain()
                    src, dst = dst, src
                    step //= 2
                size *= 2
            nc.vector.tensor_copy(dst[:], src[:]).then_inc(is_sorted, 1)

        @block.sync
        def _(sp):
            sp.wait_ge(is_sorted, 1)
            for pair in range(BP):
                sp.dma_start(d["sorted"][2 * pair:2 * pair + 2].rearrange("b c n -> (b c) n"),
                             keys[(STEPS + 1) % 2][:, pair * S.N:(pair + 1) * S.N]).then_inc(stored, 16)
            sp.wait_ge(stored, 16 * BP)


SLOTS = (0, 64, 32, 32, 32, 32, 32, 32)


def thin_phase(nc, S, d, sb):
    with ExitStack() as ctx:
        buf = lambda n, s, dt=FP32: ctx.enter_context(nc.sbuf_tensor(n, s, dt))
        sem = lambda n: ctx.enter_context(nc.semaphore(n))
        Q = len(TAUS)
        adj_t = [buf(f"cadj{u}", [P, S.N]) for u in range(2)]
        keep = buf("keep", [P, S.T, S.N], BF16)
        rem = buf("rem", [P, S.T, S.N], BF16)
        rank = buf("rank", [P, S.T, S.N], FP16)
        nearT = buf("tnearT", [P, S.T, S.N], BF16)
        deg, odd, skip, first, second = (buf(n, [P, S.T]) for n in ("deg", "odd", "skip", "first", "second"))
        deg_i = buf("deg_i", [P, S.T], INT32)
        load = buf("load", [P, S.B, S.T])
        top = buf("top", [P, 1])
        top1 = buf("top1", [1, 1])
        ps = ctx.enter_context(nc.psum_tensor("ps_thin", [P, 8 * BANK], FP32))
        bank = lambda k, n=1: ps[:, k * BANK:(k + n) * BANK]
        adj_ready = [sem(f"cadj_ready{u}") for u in range(2)]
        adj_read, near_made, turned, turn_read, near_done, deg_done, deg_read, near_stored, top_done, top_turned, passed = (
            sem(n) for n in ("cadj_read", "near_made", "c_turned", "turn_read", "near_done", "deg_done", "deg_read",
                             "near_stored", "top_done", "top_turned", "tpassed"))
        block = ctx.enter_context(nc.Block())

        @block.sync
        def _(sp):
            sp.sem_inc(near_stored, 16)
            with sp.Fori(0, S.B) as b:
                for k in range(S.T):
                    sp.wait_ge(adj_read, b * S.T + k + 1)
                    sp.dma_start(adj_t[k % 2][:], d["adj"][bass.ds(b, 1), k * P:(k + 1) * P, :]
                                 .rearrange("o p n -> (o p) n")).then_inc(adj_ready[k % 2], 16)
                wait_alone(sp, near_done, b + 1, passed)
                sp.dma_start(d["near"][bass.ds(b, 1)].rearrange("o p n -> (o p) n"),
                             nearT[:].rearrange("p t n -> p (t n)")).then_inc(near_stored, 16)
            sp.wait_ge(near_stored, 16 * S.B + 16)

        @block.tensor
        def _(pe):
            with pe.Fori(0, S.B) as b:
                pe.wait_ge(near_made, b + 1)
                for k in range(S.T):
                    pe.wait_ge(turn_read, b * S.T + k + 1)
                    half = bank(k % 2).bitcast(BF16)
                    for i in range(S.T):
                        last = nc.tensor.transpose(half[:, i * P:(i + 1) * P], keep[:, i, k * P:(k + 1) * P], sb["ident_b"][:])
                    last.then_inc(turned, 1)
                pe.wait_ge(near_done, b + 1)
                pe.wait_ge(deg_read, b + 1)
                for i in range(S.T):
                    for k in range(S.T):
                        last = nc.tensor.matmul(bank(2)[:, i:i + 1], nearT[:, k, i * P:(i + 1) * P], sb["ones_b"][:, 0:1],
                                                start=(k == 0), stop=(k == S.T - 1))
                last.then_inc(deg_done, 1)
            pe.wait_ge(top_done, 1)
            nc.tensor.transpose(bank(3)[0:1, 0:P], top[:], sb["ident"][:]).then_inc(top_turned, 1)

        @block.vector
        def _(v):
            v.sem_inc(adj_read, 2)
            v.sem_inc(turn_read, 2)
            v.sem_inc(deg_read, 1)
            with v.Fori(0, S.B) as b:
                for k in range(S.T):
                    v.wait_ge(adj_ready[k % 2], (b * (S.T // 2) + k // 2) * 16 + 16)
                    nc.vector.tensor_scalar(keep[:, k, :], adj_t[k % 2][:], 0.0, None, ALU.is_gt).then_inc(adj_read, 1)
                    v.drain()
                    own_block = keep[:, k, k * P:(k + 1) * P]
                    nc.vector.tensor_tensor(own_block, own_block, sb["off_diag"][:], ALU.mult)
                    v.drain()
                    nc.vector.tensor_tensor_scan(rank[:, k, :], keep[:, k, :], keep[:, k, :], 0.0, ALU.add, ALU.max)
                v.drain()
                nc.vector.tensor_copy(deg[:], rank[:, :, S.N - 1])
                v.drain()
                nc.vector.tensor_copy(deg_i[:], deg[:])
                v.drain()
                nc.vector.tensor_scalar(deg_i[:], deg_i[:], 1, None, ALU.bitwise_and)
                v.drain()
                nc.vector.tensor_copy(odd[:], deg_i[:])
                v.drain()
                nc.vector.tensor_tensor(skip[:], deg[:], odd[:], ALU.add)
                v.drain()
                nc.vector.tensor_scalar(odd[:], deg[:], DEG_T, None, ALU.is_gt)
                v.drain()
                nc.vector.tensor_tensor(odd[:], odd[:], sb["mask"][:, bass.ds(b * S.T, S.T)], ALU.mult)
                v.drain()
                nc.vector.tensor_tensor(second[:], skip[:], odd[:], ALU.mult)
                v.drain()
                nc.vector.tensor_scalar(first[:], second[:], 0.5, None, ALU.mult)
                v.drain()
                for k in range(S.T):
                    nc.vector.tensor_scalar(rem[:, k, :], rank[:, k, :], first[:, k:k + 1], None, ALU.is_equal)
                v.drain()
                for k in range(S.T):
                    nc.vector.scalar_tensor_tensor(rem[:, k, :], rank[:, k, :], second[:, k:k + 1], rem[:, k, :],
                                                   ALU.is_equal, ALU.add)
                v.drain()
                nc.vector.tensor_tensor(rem[:], rem[:], keep[:], ALU.mult)
                v.drain()
                nc.vector.tensor_tensor(keep[:], keep[:], rem[:], ALU.subtract).then_inc(near_made, 1)
                for k in range(S.T):
                    v.wait_ge(turned, b * S.T + k + 1)
                    v.wait_ge(near_stored, b * 16 + 16)
                    nc.vector.scalar_tensor_tensor(nearT[:, k, :], rem[:, k, :], 0.0, bank(k % 2).bitcast(BF16),
                                                   ALU.is_equal, ALU.mult).then_inc(turn_read, 1)
                    v.drain()
                    own_block = nearT[:, k, k * P:(k + 1) * P]
                    last = nc.vector.tensor_tensor(own_block, own_block, sb["ident_b"][:], ALU.max)
                last.then_inc(near_done, 1)
                v.wait_ge(deg_done, b + 1)
                nc.vector.tensor_copy(sb["deg"][:, bass.ds(b * S.T, S.T)], bank(2)[:, 0:S.T]).then_inc(deg_read, 1)
            v.drain()
            degs = sb["deg"][:].rearrange("p (b t) -> p b t", t=S.T)
            for k in range(S.T):
                nc.vector.tensor_scalar(load[:, :, k], degs[:, :, k], 1.0 / SLOTS[k] if SLOTS[k] else 0.0, None, ALU.mult)
            v.drain()
            nc.vector.reduce_max(top[:], load[:].rearrange("p b t -> p (b t)"), axis=AX.X).then_inc(top_done, 1)
            for q in range(Q):
                nc.vector.tensor_scalar(sb["bias"][:, :, q], sb["deg"][:], WTS[q] * TAUS[q],
                                        WTS[q] * (1.0 - TAUS[q]), ALU.mult, ALU.add)
            v.wait_ge(top_turned, 1)
            nc.vector.reduce_max(top1[:], bank(3)[0:1, 0:P], axis=AX.X)
            v.drain()
            nc.vector.tensor_scalar(sb["fits"][:], top1[:], 1.0, None, ALU.is_le)


def end_of_graph(nc, S, d, sb, B, X):
    ps = B["ps"]
    bank = lambda k, n=1: ps[:, k * BANK:(k + n) * BANK]
    HALVES = S.N // BANK

    def tensor(pe, b):
        wait_alone(pe, X["mix_done"], b + 1, X["passed"])
        for k in range(S.T):
            last = nc.tensor.transpose(ps[0:S.C, k * P:(k + 1) * P], B["mix"][:, k, :], sb["ident"][:])
        last.then_inc(X["mixT_done"], 1)
        pe.wait_ge(X["mixT_read"], b + 1)
        for half in range(HALVES):
            last = nc.tensor.matmul(bank(2 + half)[0:S.HID, :], sb["w1"][:], B["mixT"][:, half * BANK:(half + 1) * BANK],
                                    start=True, stop=True)
        last.then_inc(X["hid_done"], 1)
        pe.wait_ge(X["hid_read"], b + 1)
        for k in range(S.T):
            last = nc.tensor.matmul(bank(4)[:, k * S.C:(k + 1) * S.C], B["hidT"][:, k * P:(k + 1) * P], sb["w2"][:],
                                    start=True, stop=True)
        last.then_inc(X["y_done"], 1)

    def scalar(act, b):
        act.wait_ge(X["hid_done"], b + 1)
        nc.scalar.activation(B["hidT"][:], bank(2, 2)[0:S.HID, :], ACT.Relu, bias=sb["b1"][:]).then_inc(X["hid_read"], 1)

    def vector(v, b):
        res = B["res"]
        v.wait_ge(X["mixT_done"], b + 1)
        nc.vector.tensor_copy(B["mixT"][:], ps[0:S.C, 0:S.N]).then_inc(X["mixT_read"], 1)
        v.wait_ge(X["y_done"], b + 1)
        v.wait_ge(X["out_stored"], b * 16 + 16)
        nc.vector.tensor_tensor(res[:], bank(4)[:, 0:S.T * S.C].rearrange("p (t c) -> p t c", c=S.C),
                                sb["b2"][:][:, None, :].to_broadcast([P, S.T, S.C]), ALU.add)
        v.drain()
        nc.vector.tensor_tensor(res[:], res[:], sb["mask"][:, bass.ds(b * S.T, S.T)][:, :, None]
                                .to_broadcast([P, S.T, S.C]), ALU.mult)
        v.drain()
        nc.vector.tensor_tensor(res[:], res[:], sb["x1"][:, :, bass.ds(b, 1), :].rearrange("p t o c -> p (t o) c"),
                                ALU.add).then_inc(X["res_done"], 1)

    def sync(sp, b):
        wait_alone(sp, X["res_done"], b + 1, X["passed"])
        sp.dma_start(d["out"][bass.ds(b, 1)].rearrange("o (t p) c -> p (o t) c", p=P),
                     B["res"][:]).then_inc(X["out_stored"], 16)

    return tensor, scalar, vector, sync


def counting_program(nc, S, d, sb, B, X):
    Q, CB, HALVES = len(TAUS), 4, S.N // BANK
    ps = B["ps"]
    bank = lambda k, n=1: ps[:, k * BANK:(k + n) * BANK]
    level, gap, below, own, ramp, nearT = (B[n] for n in ("level", "gap", "below", "own", "ramp", "nearT"))
    agg, mix = B["agg"], B["mix"]
    last_tensor, last_scalar, last_vector, last_sync = end_of_graph(nc, S, d, sb, B, X)

    def sync(sp):
        sp.sem_inc(X["out_stored"], 16)
        with sp.Fori(0, S.B) as b:
            wait_alone(sp, X["near_free"], b + 1, X["passed"])
            sp.dma_start(nearT[:].rearrange("p t n -> p (t n)"), d["near"][bass.ds(b, 1)]
                         .rearrange("o p n -> (o p) n")).then_inc(X["near_ready"], 16)
            with sp.Fori(0, S.C // 2) as c2:
                for w in range(2):
                    sp.wait_ge(X["below_done"], b * S.C + c2 * 2 + w + 1)
                    sp.dma_start(level[w][:], d["sorted"][bass.ds(b, 1), bass.ds(c2 * 2 + w, 1), :]
                                 .rearrange("o c n -> (o c) n").to_broadcast([P, S.N])).then_inc(X["level_ready"][w], 16)
            last_sync(sp, b)
        sp.wait_ge(X["out_stored"], 16 * S.B + 16)

    def gpsimd(pool):
        pool.sem_inc(X["below_done"], 2)
        with pool.Fori(0, S.B) as b:
            with pool.Fori(0, S.C // 2) as c2:
                for w in range(2):
                    c = b * S.C + c2 * 2 + w
                    pool.wait_ge(X["counted"], (c + 1) * S.T)
                    nc.gpsimd.tensor_copy(own[w][:], sb["h"][:, :, bass.ds(b, 1), bass.ds(c2 * 2 + w, 1)]
                                          .rearrange("p t o c -> p (t o c)")).then_inc(X["own_copied"], 1)
                    pool.wait_ge(X["summed"], (c + 1) * S.T)
                    pool.wait_ge(X["own_copied"], c + 1)
                    wait_alone(pool, X["level_ready"][w], (b * (S.C // 2) + c2) * 16 + 16, X["passed"])
                    for k in range(S.T):
                        nc.gpsimd.tensor_scalar(below[w][:, k, :], level[w][:], own[w][:, k:k + 1], None, ALU.is_gt)
                    nc.gpsimd.tensor_tensor(gap[w][:, 1:], level[w][:, 1:], level[w][:, :-1], ALU.subtract)
                    nc.gpsimd.tensor_copy(gap[w][:, 0:1], level[w][:, 0:1])
                    pool.drain().then_inc(X["below_done"], 1)

    def tensor(pe):
        pe.sem_inc(X["counted"], 2 * S.T)
        with pe.Fori(0, S.B) as b:
            with pe.Fori(0, S.C // 2) as c2:
                pe.wait_ge(X["near_ready"], b * 16 + 16)
                for w in range(2):
                    c = b * S.C + c2 * 2 + w
                    pe.wait_ge(X["below_done"], c + 3)
                    for i in range(S.T):
                        pe.wait_ge(X["ramped"], c * S.T + i + 1)
                        for half in range(HALVES):
                            for k in range(S.T):
                                last = nc.tensor.matmul(bank(2 * (i % CB) + half), nearT[:, k, i * P:(i + 1) * P],
                                                        below[w][:, k, half * BANK:(half + 1) * BANK],
                                                        start=(k == 0), stop=(k == S.T - 1))
                        last.then_inc(X["counted"], 1)
            last_tensor(pe, b)

    def scalar(act):
        act.sem_inc(X["ramped"], CB)
        with act.Fori(0, S.B) as b:
            nc.scalar.copy(B["bias_b"][:], sb["bias"][:, bass.ds(b * S.T, S.T), :])
            act.drain()
            with act.Fori(0, S.C // 2) as c2:
                for w in range(2):
                    for i in range(S.T):
                        g = (b * S.C + c2 * 2 + w) * S.T + i
                        act.wait_ge(X["counted"], g + 1 + 2 * S.T)
                        act.wait_ge(X["summed"], g + S.T * 2 - 1)
                        for q in range(Q):
                            last = nc.scalar.activation(ramp[i % 2][:, q, :], bank(2 * (i % CB), 2), ACT.Relu,
                                                        bias=B["bias_b"][:, i, q:q + 1], scale=-WTS[q])
                        last.then_inc(X["ramped"], 1)
            last_scalar(act, b)

    def vector(v):
        v.sem_inc(X["summed"], 2 * S.T)
        v.sem_inc(X["near_free"], 1)
        with v.Fori(0, S.B) as b:
            with v.Fori(0, S.C // 2) as c2:
                for w in range(2):
                    for i in range(S.T):
                        g = (b * S.C + c2 * 2 + w) * S.T + i
                        v.wait_ge(X["ramped"], g + 1 + CB)
                        for q in range(Q):
                            last = nc.vector.scalar_tensor_tensor(
                                ramp[i % 2][:, q, :], ramp[i % 2][:, q, :], WTS[q], gap[w][:], ALU.min, ALU.mult,
                                accum_out=agg[:, i, q, bass.ds(c2 * 2 + w, 1)])
                        last.then_inc(X["summed"], 1)
            v.drain().then_inc(X["near_free"], 1)
            nc.vector.tensor_tensor(mix[:], agg[:, :, 0, :], agg[:, :, 1, :], ALU.add)
            v.drain()
            nc.vector.tensor_tensor(mix[:], mix[:], agg[:, :, 2, :], ALU.add)
            v.drain()
            nc.vector.tensor_tensor(mix[:], mix[:], sb["h"][:, :, bass.ds(b, 1), :].rearrange("p t o c -> p (t o) c"),
                                    ALU.add).then_inc(X["mix_done"], 1)
            last_vector(v, b)

    return dict(sync=sync, gpsimd=gpsimd, tensor=tensor, scalar=scalar, vector=vector)


BIG = 2.0 ** 100


def slots_program(nc, S, d, sb, B, X):
    Q, CB, HALVES = len(TAUS), 4, S.N // BANK
    ps = B["ps"]
    bank = lambda k, n=1: ps[:, k * BANK:(k + n) * BANK]
    level, gap, below, own, ramp, nearT = (B[n] for n in ("level", "gap", "below", "own", "ramp", "nearT"))
    mix, order, vals, tmp, hot, parts, agg0, aggs, own_bias, wts, fit = (
        B[n] for n in ("mix", "order", "vals", "tmp", "hot", "parts", "agg0", "aggs", "own_bias", "wts", "fit"))
    rest = B["rest"]
    last_tensor, last_scalar, last_vector, last_sync = end_of_graph(nc, S, d, sb, B, X)
    BY_VECTOR, BY_SCALAR, BY_POOL = range(0, 4), range(4, 7), range(7, 8)
    C2 = S.C // 2
    G = 2
    SB = BANK // S.C
    GROUPS = sum(SLOTS) // G
    BANKS = sum(SLOTS) // SB
    TILES = S.T - 1
    D1, D2 = SLOTS[1], SLOTS[2]

    def sync(sp):
        sp.sem_inc(X["out_stored"], 16)
        with sp.Fori(0, S.B) as b:
            wait_alone(sp, X["near_free"], b + 1, X["passed"])
            sp.dma_start(nearT[:].rearrange("p t n -> p (t n)"), d["near"][bass.ds(b, 1)]
                         .rearrange("o p n -> (o p) n")).then_inc(X["near_ready"], 16)
            with sp.Fori(0, C2) as c2:
                for w in range(2):
                    c = b * S.C + c2 * 2 + w
                    sp.wait_ge(X["below_p"], c + 1)
                    sp.wait_ge(X["below_v"], c + 1)
                    wait_alone(sp, X["below_a"], c + 1, X["passed"])
                    sp.dma_start(level[w][:], d["sorted"][bass.ds(b, 1), bass.ds(c2 * 2 + w, 1), :]
                                 .rearrange("o c n -> (o c) n").to_broadcast([P, S.N])).then_inc(X["level_ready"][w], 16)
            last_sync(sp, b)
        sp.wait_ge(X["out_stored"], 16 * S.B + 16)

    def gpsimd(pool):
        pool.sem_inc(X["below_p"], 2)
        with pool.Fori(0, S.B) as b:
            with pool.Fori(0, C2) as c2:
                for w in range(2):
                    c = b * S.C + c2 * 2 + w
                    pool.wait_ge(X["below_v"], c + 1)
                    pool.wait_ge(X["below_a"], c + 1)
                    nc.gpsimd.tensor_copy(own[w][:], sb["h"][:, :, bass.ds(b, 1), bass.ds(c2 * 2 + w, 1)]
                                          .rearrange("p t o c -> p (t o c)")).then_inc(X["own_copied"], 1)
                    wait_alone(pool, X["own_copied"], c + 1, X["passed"])
                    nc.gpsimd.tensor_scalar(own_bias[w][:], own[w][:], 1.0 + 2.0 ** -23, 1.0 / BIG, ALU.mult, ALU.max)
                    pool.drain()
                    nc.gpsimd.tensor_scalar(own_bias[w][:], own_bias[w][:], -BIG, 0.0, ALU.mult, ALU.add)
                    pool.drain().then_inc(X["own_done"], 1)
                    pool.wait_ge(X["counted"], c + 1)
                    pool.wait_ge(X["summed"], c + 1)
                    wait_alone(pool, X["level_ready"][w], (b * C2 + c2) * 16 + 16, X["passed"])
                    for k in BY_POOL:
                        nc.gpsimd.tensor_scalar(below[w][:, k, :], level[w][:], own[w][:, k:k + 1], None, ALU.is_gt)
                    nc.gpsimd.tensor_tensor(gap[w][:, 1:], level[w][:, 1:], level[w][:, :-1], ALU.subtract)
                    nc.gpsimd.tensor_copy(gap[w][:, 0:1], level[w][:, 0:1])
                    pool.drain().then_inc(X["below_p"], 1)

    def tensor(pe):
        pe.sem_inc(X["counted"], 2)
        pe.sem_inc(X["hot_used"], 2)

        def gather(base, bank0, slots):
            g0, v0 = base
            for s in range(0, slots, G):
                g = g0 + s // G
                pe.wait_ge(X["hot_done"], g + 1)
                if s % SB == 0:
                    pe.wait_ge(X["vals_read"], v0 + s // SB + 1)
                for u in range(G):
                    o = bank(bank0 + s // SB)[:, (s % SB + u) * S.C:(s % SB + u + 1) * S.C]
                    for k in range(S.T):
                        for part in range(3):
                            last = nc.tensor.matmul(o, hot[(s // G) % 2][:, u, k, :], parts[:, k, part, :],
                                                    start=(k == 0 and part == 0), stop=(k == S.T - 1 and part == 2))
                last.then_inc(X["hot_used"], 1)

        with pe.Fori(0, S.B) as b:
            for k in range(S.T):
                pe.wait_ge(X["order_read"], b * S.T + k + 1)
                pe.wait_ge(X["near_ready"], b * 16 + 16)
                for half in range(HALVES):
                    for j in range(k + 1):
                        last = nc.tensor.matmul(bank(2 * (k % 2) + half), (sb["ones_b"] if j < k else sb["upto_b"])[:],
                                                nearT[:, j, half * BANK:(half + 1) * BANK],
                                                start=(j == 0), stop=(j == k))
                last.then_inc(X["order_done"], 1)
            with pe.Fori(0, C2) as c2:
                pe.wait_ge(X["order_read"], b * S.T + S.T + 2)
                for w in range(2):
                    c = b * S.C + c2 * 2 + w
                    for name in ("below_p", "below_v", "below_a"):
                        pe.wait_ge(X[name], c + 3)
                    pe.wait_ge(X["ramped"], c + 1)
                    for half in range(HALVES):
                        for k in range(S.T):
                            last = nc.tensor.matmul(bank(2 * w + half), nearT[:, k, 0:P],
                                                    below[w][:, k, half * BANK:(half + 1) * BANK],
                                                    start=(k == 0), stop=(k == S.T - 1))
                    last.then_inc(X["counted"], 1)
            wait_alone(pe, X["ramped"], b * S.C + S.C + 2, X["passed"])
            gather((b * GROUPS, b * BANKS), 0, D1)
            with pe.Fori(0, TILES // 2) as t2:
                for u in range(2):
                    t = t2 * 2 + u
                    gather((b * GROUPS + D1 // G + t * (D2 // G), b * BANKS + D1 // SB + t * (D2 // SB)),
                           u * (D2 // SB), D2)
            last_tensor(pe, b)

    def scalar(act):
        act.sem_inc(X["below_a"], 2)
        act.sem_inc(X["ramped"], 2)
        act.sem_inc(X["vals_read"], 8)

        def compare(b, c2, w):
            c = b * S.C + c2 * 2 + w
            act.wait_ge(X["own_done"], c + 1)
            act.wait_ge(X["counted"], c + 1)
            act.wait_ge(X["level_ready"][w], (b * C2 + c2) * 16 + 16)
            for k in BY_SCALAR:
                last = nc.scalar.activation(below[w][:, k, :], level[w][:], ACT.Sigmoid, bias=own_bias[w][:, k:k + 1], scale=BIG)
            last.then_inc(X["below_a"], 1)

        def ramps(b, c2, w):
            c = b * S.C + c2 * 2 + w
            act.wait_ge(X["counted"], c + 3)
            act.wait_ge(X["summed"], c + 1)
            for q in range(Q):
                last = nc.scalar.activation(ramp[w][:, q, :], bank(2 * w, 2), ACT.Relu,
                                            bias=B["bias_b"][:, 0, q:q + 1], scale=-WTS[q])
            last.then_inc(X["ramped"], 1)

        def take(base, v_free, bank0, slots):
            for k in range(slots // SB):
                act.wait_ge(X["hot_used"], base + (k + 1) * (SB // G) + 2)
                act.wait_ge(X["vals_free"], v_free)
                nc.scalar.copy(vals[:, k * SB * S.C:(k + 1) * SB * S.C], bank(bank0 + k)).then_inc(X["vals_read"], 1)

        with act.Fori(0, S.B) as b:
            nc.scalar.copy(B["bias_b"][:], sb["bias"][:, bass.ds(b * S.T, S.T), :])
            act.drain()
            compare(b, 0, 0)
            with act.Fori(0, C2 - 1) as c2:
                compare(b, c2, 1)
                ramps(b, c2, 0)
                compare(b, c2 + 1, 0)
                ramps(b, c2, 1)
            compare(b, C2 - 1, 1)
            ramps(b, C2 - 1, 0)
            ramps(b, C2 - 1, 1)
            take(b * GROUPS, b * TILES + 1, 0, D1)
            with act.Fori(0, TILES // 2) as t2:
                for u in range(2):
                    t = t2 * 2 + u
                    take(b * GROUPS + D1 // G + t * (D2 // G), b * TILES + t + 2, u * (D2 // SB), D2)
            last_scalar(act, b)

    def vector(v):
        v.sem_inc(X["below_v"], 2)
        v.sem_inc(X["summed"], 2)
        v.sem_inc(X["near_free"], 1)
        v.sem_inc(X["order_read"], 2)
        v.sem_inc(X["vals_free"], 1)

        def compare(b, c2, w):
            c = b * S.C + c2 * 2 + w
            v.wait_ge(X["own_done"], c + 1)
            v.wait_ge(X["counted"], c + 1)
            v.wait_ge(X["level_ready"][w], (b * C2 + c2) * 16 + 16)
            for k in BY_VECTOR:
                last = nc.vector.tensor_scalar(below[w][:, k, :], level[w][:], own[w][:, k:k + 1], None, ALU.is_gt)
            last.then_inc(X["below_v"], 1)

        def sums(b, c2, w):
            c = b * S.C + c2 * 2 + w
            v.wait_ge(X["ramped"], c + 3)
            v.wait_ge(X["below_p"], c + 3)
            for q in range(Q):
                last = nc.vector.scalar_tensor_tensor(
                    ramp[w][:, q, :], ramp[w][:, q, :], WTS[q], gap[w][:], ALU.min, ALU.mult,
                    accum_out=agg0[:, q, bass.ds(c2 * 2 + w, 1)])
            last.then_inc(X["summed"], 1)

        def one_hots(base, t, slots):
            for s in range(0, slots, G):
                v.wait_ge(X["hot_used"], base + s // G + 1)
                for u in range(G):
                    last = nc.vector.tensor_scalar(hot[(s // G) % 2][:, u, :, :], order[:, :, bass.ds(t * P, P)],
                                                   float(s + u + 1), None, ALU.is_equal)
                last.then_inc(X["hot_done"], 1)

        def sort_sum(vbase, t, slots):
            v.wait_ge(X["vals_read"], vbase + slots // SB + 8)
            C, E = S.C, slots * S.C
            src, dst = vals[:, 0:E], tmp[:, 0:E]
            size = 2
            while size <= slots:
                a, o = (x.rearrange("p (n k c) -> p n k c", k=size, c=C) for x in (src, dst))
                half = size // 2
                lo, hi = a[:, :, 0:half, :], a[:, :, size - 1:half - 1:-1, :]
                nc.vector.tensor_tensor(o[:, :, 0:half, :], lo, hi, ALU.min)
                nc.vector.tensor_tensor(o[:, :, size - 1:half - 1:-1, :], lo, hi, ALU.max)
                v.drain()
                src, dst = dst, src
                step = size // 4
                while step:
                    a, o = (x.rearrange("p (n two k) -> p n two k", two=2, k=step * C) for x in (src, dst))
                    nc.vector.tensor_tensor(o[:, :, 0, :], a[:, :, 0, :], a[:, :, 1, :], ALU.min)
                    nc.vector.tensor_tensor(o[:, :, 1, :], a[:, :, 0, :], a[:, :, 1, :], ALU.max)
                    v.drain()
                    src, dst = dst, src
                    step //= 2
                size *= 2
            w = wts[:, bass.ds(t, 1), 0:slots].rearrange("p o s -> p (o s)")
            nc.vector.tensor_tensor(dst.rearrange("p (s c) -> p s c", c=C), src.rearrange("p (s c) -> p s c", c=C),
                                    w[:, :, None].to_broadcast([P, slots, C]), ALU.mult)
            v.drain()
            nc.vector.reduce_sum(aggs[:, bass.ds(t, 1), :].rearrange("p o c -> p (o c)"),
                                 dst.rearrange("p (s c) -> p c s", c=C), axis=AX.X).then_inc(X["vals_free"], 1)

        for k in range(1, S.T):
            nc.vector.memset(fit[:, k:k + 1], float(SLOTS[k]))
        nc.vector.memset(fit[:, 0:1], float(D2))
        with v.Fori(0, S.B) as b:
            hb = sb["h"][:, :, bass.ds(b, 1), :].rearrange("p t o c -> p (t o) c")
            nc.vector.tensor_copy(parts[:, :, 0, :], hb)
            v.drain()
            nc.vector.tensor_tensor(rest[:], hb, parts[:, :, 0, :], ALU.subtract)
            v.drain()
            nc.vector.tensor_copy(parts[:, :, 1, :], rest[:])
            v.drain()
            nc.vector.tensor_tensor(rest[:], rest[:], parts[:, :, 1, :], ALU.subtract)
            v.drain()
            nc.vector.tensor_copy(parts[:, :, 2, :], rest[:])
            n = sb["deg"][:, bass.ds(b * S.T, S.T)]
            at, off, off2 = B["at"], B["off"], B["off2"]
            for q in range(Q):
                v.drain()
                nc.vector.tensor_scalar(at[:], n, TAUS[q] - 1.0, -TAUS[q], ALU.mult, ALU.add)
                v.drain()
                nc.vector.tensor_tensor(at[:], at[:], fit[:], ALU.add)
                v.drain()
                nc.vector.tensor_tensor(off[:], sb["slot"][:][:, None, :].to_broadcast([P, S.T, D1]),
                                        at[:][:, :, None].to_broadcast([P, S.T, D1]), ALU.subtract)
                v.drain()
                nc.vector.tensor_scalar(off2[:], off[:], -1.0, None, ALU.mult)
                v.drain()
                nc.vector.tensor_tensor(off[:], off[:], off2[:], ALU.min)
                v.drain()
                nc.vector.tensor_scalar(off[:], off[:], 1.0, 0.0, ALU.add, ALU.max)
                v.drain()
                if q == 0:
                    nc.vector.tensor_scalar(wts[:], off[:], WTS[q], None, ALU.mult)
                else:
                    nc.vector.scalar_tensor_tensor(wts[:], off[:], WTS[q], wts[:], ALU.mult, ALU.add)
            for k in range(S.T):
                v.wait_ge(X["order_done"], b * S.T + k + 1)
                nc.vector.tensor_tensor(order[:, k, :], bank(2 * (k % 2), 2), nearT[:, k, :], ALU.mult)\
                    .then_inc(X["order_read"], 1)
            v.drain()
            compare(b, 0, 0)
            with v.Fori(0, C2 - 1) as c2:
                compare(b, c2, 1)
                sums(b, c2, 0)
                compare(b, c2 + 1, 0)
                sums(b, c2, 1)
            compare(b, C2 - 1, 1)
            sums(b, C2 - 1, 0)
            sums(b, C2 - 1, 1)
            v.drain().then_inc(X["near_free"], 1)
            nc.vector.tensor_tensor(aggs[:, 0, :], agg0[:, 0, :], agg0[:, 1, :], ALU.add)
            v.drain()
            nc.vector.tensor_tensor(aggs[:, 0, :], aggs[:, 0, :], agg0[:, 2, :], ALU.add)
            one_hots(b * GROUPS, 1, D1)
            one_hots(b * GROUPS + D1 // G, 2, D2)
            sort_sum(b * BANKS, 1, D1)
            with v.Fori(2, S.T - 1) as t:
                one_hots(b * GROUPS + D1 // G + (t - 1) * (D2 // G), t + 1, D2)
                sort_sum(b * BANKS + D1 // SB + (t - 2) * (D2 // SB), t, D2)
            sort_sum(b * BANKS + D1 // SB + (S.T - 3) * (D2 // SB), S.T - 1, D2)
            v.drain()
            nc.vector.tensor_tensor(mix[:], aggs[:], sb["h"][:, :, bass.ds(b, 1), :].rearrange("p t o c -> p (t o) c"),
                                    ALU.add).then_inc(X["mix_done"], 1)
            last_vector(v, b)

    return dict(sync=sync, gpsimd=gpsimd, tensor=tensor, scalar=scalar, vector=vector)


def aggregate_phase(nc, S, d, sb):
    with ExitStack() as ctx:
        buf = lambda n, s, dt=FP32: ctx.enter_context(nc.sbuf_tensor(n, s, dt))
        sem = lambda n: ctx.enter_context(nc.semaphore(n))
        Q, D1 = len(TAUS), max(SLOTS)
        B = dict(
            nearT=buf("nearT", [P, S.T, S.N], BF16),
            level=[buf(f"level{w}", [P, S.N]) for w in range(2)],
            gap=[buf(f"gap{w}", [P, S.N]) for w in range(2)],
            below=[buf(f"below{w}", [P, S.T, S.N], BF16) for w in range(2)],
            own=[buf(f"own{w}", [P, S.T]) for w in range(2)],
            ramp=[buf(f"ramp{w}", [P, Q, S.N], BF16) for w in range(2)],
            bias_b=buf("bias_b", [P, S.T, Q]),
            mix=buf("mix", [P, S.T, S.C]), res=buf("res", [P, S.T, S.C]),
            ps=ctx.enter_context(nc.psum_tensor("ps_agg", [P, 8 * BANK], FP32)),
        )
        B["mixT"], B["hidT"] = B["gap"][0][0:S.C, :], B["gap"][1][0:S.HID, :]
        counting, slots = dict(B), dict(B)
        with ExitStack() as other:
            counting["agg"] = other.enter_context(nc.sbuf_tensor("agg", [P, S.T, Q, S.C], FP32))
        slots.update(
            order=buf("order", [P, S.T, S.N], FP16),
            vals=buf("vals_s", [P, D1 * S.C]), tmp=buf("tmp_s", [P, D1 * S.C]),
            hot=[buf(f"hot{u}", [P, 2, S.T, P], BF16) for u in range(2)],
            parts=buf("parts", [P, S.T, 3, S.C], BF16), rest=buf("rest", [P, S.T, S.C]),
            agg0=buf("agg0", [P, Q, S.C]), aggs=buf("aggs", [P, S.T, S.C]),
            own_bias=[buf(f"own_bias{w}", [P, S.T]) for w in range(2)],
            wts=buf("wts", [P, S.T, D1]), fit=buf("fit", [P, S.T]), at=buf("at", [P, S.T]),
            off=buf("off", [P, S.T, D1]), off2=buf("off2", [P, S.T, D1]),
        )
        last = ("mix_done", "mixT_done", "mixT_read", "hid_done", "hid_read", "y_done", "res_done", "out_stored",
                "near_ready", "near_free", "counted", "ramped", "summed", "own_copied", "passed")
        XC = {n: sem("cnt_" + n) for n in last + ("below_done",)}
        XS = {n: sem("slt_" + n) for n in last + ("below_p", "below_v", "below_a", "own_done", "order_done", "order_read",
                                                  "hot_done", "hot_used", "vals_read", "vals_free")}
        XC["level_ready"] = [sem(f"cnt_level_ready{w}") for w in range(2)]
        XS["level_ready"] = [sem(f"slt_level_ready{w}") for w in range(2)]
        by_counting = counting_program(nc, S, d, sb, counting, XC)
        by_slots = slots_program(nc, S, d, sb, slots, XS)
        block = ctx.enter_context(nc.Block())

        def either(eng, name):
            fits = eng.value_load(sb["fits"][0:1, 0:1], min_val=0, max_val=1)
            with eng.If(fits > 0):
                by_slots[name](eng)
            with eng.Else():
                by_counting[name](eng)

        @block.sync
        def _(sp):
            either(sp, "sync")

        @block.gpsimd
        def _(pool):
            either(pool, "gpsimd")

        @block.tensor
        def _(pe):
            either(pe, "tensor")

        @block.scalar
        def _(act):
            either(act, "scalar")

        @block.vector
        def _(v):
            either(v, "vector")


def build(nc, x, adj, mask, w_qkv, w_proj, b_proj, w_gamma, b_gamma, w1, b1, w2, b2, out):
    S = Shapes(x, w_qkv, w1)
    d = dict(x=x, adj=adj, mask=mask, w_qkv=w_qkv, w_proj=w_proj, b_proj=b_proj, w_gamma=w_gamma,
             b_gamma=b_gamma, w1=w1, b1=b1, w2=w2, b2=b2, out=out)
    d["near"] = nc.dram_tensor("near_adjacency", [S.B, P, S.T * S.N], BF16).ap()
    d["sorted"] = nc.dram_tensor("sorted_levels", [S.B, S.C, S.N], FP32).ap()
    with ExitStack() as ctx:
        sb = {}
        for name, shape, dt in (
            ("x1", [P, S.T, S.B, S.C], FP32),
            ("h", [P, S.T, S.B, S.C], FP32),
            ("ident", [P, P], FP32), ("ones", [P, P], FP32), ("off_diag", [P, P], FP32),
            ("ident_b", [P, P], BF16), ("ones_b", [P, P], BF16), ("upto_b", [P, P], BF16),
            ("slot", [P, max(SLOTS)], FP32),
            ("deg", [P, S.B * S.T], FP32),
            ("bias", [P, S.B * S.T, len(TAUS)], FP32),
            ("fits", [1, 1], INT32),
            ("wqkvT", [S.C, 3 * S.F], FP32), ("wprojT", [P, S.F // P, S.C], FP32),
            ("wgam", [S.C, 2], FP32), ("wgam0", [S.C, P], FP32), ("bgam", [P, 2], FP32), ("bproj", [P, S.C], FP32),
            ("w1", [S.C, S.HID], FP32), ("b1", [S.HID, 1], FP32), ("w2", [S.HID, S.C], FP32), ("b2", [P, S.C], FP32),
            ("mask", [P, S.B * S.T], FP32),
        ):
            sb[name] = ctx.enter_context(nc.sbuf_tensor("k_" + name, shape, dt))
        setup_phase(nc, S, d, sb)
        attention_phase(nc, S, d, sb)
        sort_phase(nc, S, d, sb)
        thin_phase(nc, S, d, sb)
        aggregate_phase(nc, S, d, sb)


_INS = ["x", "adj", "nodemask", "L0_gnn_W_qkv", "L0_gnn_W_proj", "L0_gnn_b_proj", "L0_gnn_W_gamma", "L0_gnn_b_gamma",
        "L1_gnn_W1", "L1_gnn_b1", "L1_gnn_W2", "L1_gnn_b2"]


def kernel(**inputs):
    import numpy as np
    import concourse.bacc as bacc
    from concourse.bass_utils import run_bass_kernel_spmd

    nc = bacc.Bacc("TRN2", target_bir_lowering=False, num_devices=1)
    arrays, args = {}, []
    for name in _INS:
        a = np.ascontiguousarray(inputs[name])
        if a.dtype == np.bool_:
            a = a.view(np.uint8)
        arrays[f"in_{name}"] = a
        args.append(nc.dram_tensor(f"in_{name}", a.shape, mybir.dt.from_np(a.dtype), kind="ExternalInput").ap())
    shape = tuple(np.shape(inputs["x"]))
    out = nc.dram_tensor("out_x", shape, FP32, kind="ExternalOutput").ap()
    build(nc, *args, out)
    r = run_bass_kernel_spmd(nc, [arrays], core_ids=[0])
    return r.results[0]["out_x"]
```

```python
import concourse.bass as bass
from concourse import mybir
from contextlib import ExitStack

FP32 = mybir.dt.float32
BF16 = mybir.dt.bfloat16
FP16 = mybir.dt.float16
INT32 = mybir.dt.int32
UINT8 = mybir.dt.uint8
ALU = mybir.AluOpType
ACT = mybir.ActivationFunctionType
AX = mybir.AxisListType

P = 128
BANK = 512


class Shapes:

    def __init__(self, x, w_qkv, w1):
        self.B, self.N, self.C = x.shape
        self.T = self.N // P
        self.F = w_qkv.shape[0] // 3
        self.D = self.C
        self.H = self.F // self.D
        self.HP = self.H // 2
        self.HID = w1.shape[1]


TAUS = (0.25, 0.5, 0.75)
WTS = (0.25, 0.5, 0.25)
DEG_T = 10.0
EPS = 1e-5


def wait_alone(eng, sem, value, passed):
    eng.wait_ge(sem, value)
    eng.sem_inc(passed, 1)


def layer_norm_relu(nc, x, h, tmp, mean, var, y, t):
    v = nc.vector
    G, C = x.shape[1], x.shape[2]
    v.reduce_sum(mean, x, axis=AX.X)
    v.drain()
    v.tensor_scalar(mean, mean, 1.0 / C, None, ALU.mult)
    v.drain()
    v.tensor_tensor(h, x, mean[:, :, None].to_broadcast([P, G, C]), ALU.subtract)
    v.drain()
    v.tensor_tensor(tmp, h, h, ALU.mult)
    v.drain()
    v.reduce_sum(var, tmp, axis=AX.X)
    v.drain()
    v.tensor_scalar(var, var, 1.0 / C, EPS, ALU.mult, ALU.add)
    v.drain()
    v.tensor_scalar(t.bitcast(INT32), var.bitcast(INT32), 1, None, ALU.logical_shift_right)
    v.drain()
    v.tensor_scalar(y.bitcast(INT32), t.bitcast(INT32), -1.0, 1597463007.0, ALU.mult, ALU.add)
    v.drain()
    for _ in range(4):
        v.tensor_tensor(t, y, y, ALU.mult)
        v.drain()
        v.tensor_tensor(t, t, var, ALU.mult)
        v.drain()
        v.tensor_scalar(t, t, -0.5, 1.5, ALU.mult, ALU.add)
        v.drain()
        v.tensor_tensor(y, y, t, ALU.mult)
        v.drain()
    v.tensor_tensor(tmp, h, y[:, :, None].to_broadcast([P, G, C]), ALU.mult)
    v.drain()
    return v.tensor_scalar(h, tmp, 0.0, None, ALU.max)


def setup_phase(nc, S, d, sb):
    with ExitStack() as ctx:
        buf = lambda n, s, dt=FP32: ctx.enter_context(nc.sbuf_tensor(n, s, dt))
        sem = lambda n: ctx.enter_context(nc.semaphore(n))
        KT = 3 * S.F // P
        wqkv_rows = buf("wqkv_rows", [P, KT, S.C])
        wproj_rows = buf("wproj_rows", [S.C, S.F])
        wgam_rows = buf("wgam_rows", [2, S.C])
        mask_rows = buf("mask_rows", [S.B * S.T, P], UINT8)
        mask_rows_f = buf("mask_rows_f", [S.B * S.T, P])
        upto = buf("upto", [P, P])
        slot_i = buf("slot_i", [P, max(SLOTS)], INT32)
        tmp = buf("ln_tmp0", [P, S.T * S.B, S.C])
        mean, var, y, t = (buf(f"ln0_{n}", [P, S.T * S.B]) for n in ("mean", "var", "y", "t"))
        ps = ctx.enter_context(nc.psum_tensor("ps_setup", [P, 8 * BANK], FP32))
        loaded_x, loaded_w, ident_done, ones_done = sem("su_x"), sem("su_w"), sem("su_id"), sem("su_one")
        copied, turned = sem("su_copied"), sem("su_turned")
        block = ctx.enter_context(nc.Block())

        @block.sync
        def _(sp):
            for b in range(S.B):
                sp.dma_start(sb["x1"][:, :, b, :], d["x"][b].rearrange("(t p) c -> p t c", p=P)).then_inc(loaded_x, 16)

        @block.scalar
        def _(act):
            for dst, src in (
                (wqkv_rows[:], d["w_qkv"].rearrange("(t p) c -> p t c", p=P)),
                (wproj_rows[:], d["w_proj"]),
                (wgam_rows[:], d["w_gamma"]),
                (mask_rows[:], d["mask"].rearrange("b (t p) -> (b t) p", p=P)),
                (sb["bproj"][:], d["b_proj"][None, :].to_broadcast([P, S.C])),
                (sb["bgam"][:], d["b_gamma"][None, :].to_broadcast([P, 2])),
                (sb["w1"][:], d["w1"]),
                (sb["b1"][:], d["b1"][:, None]),
                (sb["w2"][:], d["w2"]),
                (sb["b2"][:], d["b2"][None, :].to_broadcast([P, S.C])),
            ):
                act.dma_start(dst, src).then_inc(loaded_w, 16)

        @block.gpsimd
        def _(pool):
            nc.gpsimd.memset(sb["ident"][:], 0.0)
            nc.gpsimd.memset(sb["ones"][:], 1.0).then_inc(ones_done, 1)
            pool.wait_ge(ones_done, 1)
            nc.gpsimd.affine_select(out=sb["ident"][:], in_=sb["ident"][:], compare_op=ALU.not_equal, fill=1.0,
                                    base=0, pattern=[[-1, P]], channel_multiplier=1)
            nc.gpsimd.affine_select(out=upto[:], in_=sb["ones"][:], compare_op=ALU.is_ge, fill=0.0,
                                    base=0, pattern=[[1, P]], channel_multiplier=-1)
            nc.gpsimd.iota(slot_i[:], pattern=[[1, max(SLOTS)]], base=0, channel_multiplier=0)
            pool.drain().then_inc(ident_done, 1)

        @block.tensor
        def _(pe):
            pe.wait_ge(loaded_w, 160)
            pe.wait_ge(ident_done, 1)
            for k in range(KT):
                nc.tensor.transpose(ps[0:S.C, k * P:(k + 1) * P], wqkv_rows[:, k, :], sb["ident"][:])
            for k in range(S.F // P):
                nc.tensor.transpose(ps[:, 3 * BANK + k * S.C:3 * BANK + (k + 1) * S.C],
                                    wproj_rows[:, k * P:(k + 1) * P], sb["ident"][0:S.C, 0:S.C])
            nc.tensor.transpose(ps[0:S.C, 5 * BANK:5 * BANK + 2], wgam_rows[:], sb["ident"][0:2, 0:2])
            pe.wait_ge(copied, 1)
            nc.tensor.transpose(ps[:, 4 * BANK:4 * BANK + S.B * S.T], mask_rows_f[:],
                                sb["ident"][0:S.B * S.T, 0:S.B * S.T]).then_inc(turned, 1)

        @block.vector
        def _(v):
            v.wait_ge(loaded_w, 160)
            nc.vector.tensor_copy(mask_rows_f[:], mask_rows[:]).then_inc(copied, 1)
            v.wait_ge(ident_done, 1)
            nc.vector.tensor_copy(sb["ident_b"][:], sb["ident"][:])
            nc.vector.tensor_copy(sb["ones_b"][:], sb["ones"][:])
            nc.vector.tensor_copy(sb["upto_b"][:], upto[:])
            nc.vector.tensor_copy(sb["slot"][:], slot_i[:])
            nc.vector.tensor_scalar(sb["off_diag"][:], sb["ident"][:], -1.0, 1.0, ALU.mult, ALU.add)
            v.wait_ge(loaded_x, 16 * S.B)
            layer_norm_relu(nc, sb["x1"][:].rearrange("p t b c -> p (t b) c"), sb["h"][:].rearrange("p t b c -> p (t b) c"),
                            tmp[:], mean[:], var[:], y[:], t[:])
            v.wait_ge(turned, 1)
            nc.vector.tensor_scalar(sb["wqkvT"][:, 0:S.F], ps[0:S.C, 0:S.F], S.D ** -0.5, None, ALU.mult)
            nc.vector.tensor_copy(sb["wqkvT"][:, S.F:], ps[0:S.C, S.F:3 * S.F])
            nc.vector.tensor_copy(sb["wprojT"][:].rearrange("p k c -> p (k c)"),
                                  ps[:, 3 * BANK:3 * BANK + S.F // P * S.C])
            nc.vector.tensor_copy(sb["wgam"][:], ps[0:S.C, 5 * BANK:5 * BANK + 2])
            nc.vector.tensor_copy(sb["wgam0"][:], ps[0:S.C, 5 * BANK:5 * BANK + 1].to_broadcast([S.C, P]))
            nc.vector.tensor_copy(sb["mask"][:], ps[:, 4 * BANK:4 * BANK + S.B * S.T])


def attention_phase(nc, S, d, sb):
    with ExitStack() as ctx:
        buf = lambda n, s, dt=FP32: ctx.enter_context(nc.sbuf_tensor(n, s, dt))
        sem = lambda n: ctx.enter_context(nc.semaphore(n))
        h_b = buf("h_b", [P, S.T, S.C])
        hT = buf("hT", [S.C, S.N])
        g0 = buf("g0", [P, S.N])
        g1 = buf("g1", [P, S.T])
        kT = buf("kT", [P, S.HP, S.N])
        vals = buf("vals", [P, S.T, S.F])
        adj_t = [buf(f"adj_t{u}", [P, S.N]) for u in range(2)]
        bias_t = [buf(f"bias_t{u}", [P, S.N]) for u in range(2)]
        qT_all = buf("qT_all", [P, S.HP, S.N])
        qT = [buf(f"qT{u}", [P, S.HP, P]) for u in range(2)]
        neg = [buf(f"neg{u}", [P, S.N]) for u in range(2)]
        prob = [buf(f"prob{u}", [P, S.N]) for u in range(2)]
        probT = [buf(f"probT{u}", [P, S.T, P]) for u in range(2)]
        neg_max = [buf(f"neg_max{u}", [P, S.H]) for u in range(2)]
        row_sum = [buf(f"row_sum{u}", [P, S.H]) for u in range(2)]
        row_inv = buf("row_inv", [P, S.H])
        o_sb = buf("o_sb", [P, S.F])
        oT = buf("oT", [P, S.F // P, P])
        y_sb = buf("y_sb", [P, S.C])
        ps = ctx.enter_context(nc.psum_tensor("ps_att", [P, 8 * BANK], FP32))
        bank = lambda k, n=1: ps[:, k * BANK:(k + n) * BANK]
        PT0, OB, MB = 4, 6, 7

        adj_ready = [sem(f"adj_ready{u}") for u in range(2)]
        adj_free = sem("adj_free")
        h_ready, passed, passed_p = sem("h_ready"), sem("passed"), sem("passed_p")
        job_done, job_read_v, job_read_a = sem("job_done"), sem("job_read_v"), sem("job_read_a")
        q_ready = sem("q_ready")
        s_done, s_read = sem("s_done"), sem("s_read")
        p_done = sem("p_done")
        t_done, t_read_v, t_read_a = sem("t_done"), sem("t_read_v"), sem("t_read_a")
        pv_done, o_norm, oT_done, oT_read = sem("pv_done"), sem("o_norm"), sem("oT_done"), sem("oT_read")
        y_done, tile_done = sem("y_done"), sem("tile_done")
        block = ctx.enter_context(nc.Block())

        HALVES = S.N // BANK
        K0 = 5
        V0 = K0 + S.HP * HALVES
        Q0 = V0 + S.T
        JOBS = Q0 + S.HP * HALVES
        by_act = lambda j: 2 <= j < V0 or (V0 <= j < Q0 and j % 2 == 0)
        n_act = lambda j: sum(by_act(i) for i in range(j + 1))
        n_vec = lambda j: j + 1 - n_act(j)
        JA, JV = n_act(JOBS - 1), n_vec(JOBS - 1)

        @block.sync
        def _(sp):
            with sp.Fori(0, S.B) as b:
                with sp.Fori(0, S.T // 2) as i2:
                    for u in range(2):
                        n = b * S.T + i2 * 2 + u
                        sp.wait_ge(adj_free, n + 1)
                        sp.dma_start(adj_t[u][:], d["adj"][bass.ds(b, 1), bass.ds(i2 * (2 * P) + u * P, P), :]
                                     .rearrange("o p n -> (o p) n")).then_inc(adj_ready[u], 16)

        @block.gpsimd
        def _(pool):
            pool.sem_inc(s_done, 2 * S.H)
            with pool.Fori(0, S.B) as b:
                with pool.Fori(0, S.T // 2) as i2:
                    for u in range(2):
                        n = b * S.T + i2 * 2 + u
                        wait_alone(pool, job_read_v, b * JV + JV, passed_p)
                        pool.wait_ge(s_done, n * S.H + S.H)
                        nc.gpsimd.tensor_copy(qT[u][:], qT_all[:, :, bass.ds(i2 * (2 * P) + u * P, P)]).then_inc(q_ready, 1)

        @block.tensor
        def _(pe):
            with pe.Fori(0, S.B) as b:
                wait_alone(pe, h_ready, b + 1, passed)
                for j in range(JOBS):
                    if j >= 8:
                        if by_act(j - 8):
                            pe.wait_ge(job_read_a, b * JA + n_act(j - 8))
                        else:
                            pe.wait_ge(job_read_v, b * JV + n_vec(j - 8))
                    if j < 2:
                        for k in range(BANK // P):
                            last = nc.tensor.transpose(bank(j)[0:S.C, k * P:(k + 1) * P],
                                                       h_b[:, j * (BANK // P) + k, :], sb["ident"][:])
                        last.then_inc(job_done, 1)
                        if j == 1:
                            pe.wait_ge(job_read_v, b * JV + 2)
                    elif j < 4:
                        nc.tensor.matmul(bank(j), sb["wgam0"][:], hT[:, (j - 2) * BANK:(j - 1) * BANK],
                                         start=True, stop=True).then_inc(job_done, 1)
                    elif j == 4:
                        for k in range(S.T):
                            last = nc.tensor.matmul(bank(j)[:, 2 * k:2 * k + 2], hT[:, k * P:(k + 1) * P],
                                                    sb["wgam"][:], start=True, stop=True)
                        last.then_inc(job_done, 1)
                    elif j < V0 or j >= Q0:
                        pair, half = divmod(j - (K0 if j < V0 else Q0), HALVES)
                        first = S.F if j < V0 else 0
                        nc.tensor.matmul(bank(j % 8), sb["wqkvT"][:, first + pair * P:first + (pair + 1) * P],
                                         hT[:, half * BANK:(half + 1) * BANK],
                                         start=True, stop=True).then_inc(job_done, 1)
                    else:
                        k = j - V0
                        nc.tensor.matmul(bank(j % 8), hT[:, k * P:(k + 1) * P], sb["wqkvT"][:, 2 * S.F:3 * S.F],
                                         start=True, stop=True).then_inc(job_done, 1)

                def scores(n, u, h):
                    pe.wait_ge(s_read, n * S.H + h + 1)
                    r = (h % 2) * S.D
                    for half in range(HALVES):
                        last = nc.tensor.matmul(ps[:, (2 * (h % 2) + half) * BANK:(2 * (h % 2) + half + 1) * BANK],
                                                qT[u][r:r + S.D, h // 2, :],
                                                kT[r:r + S.D, h // 2, half * BANK:(half + 1) * BANK],
                                                start=True, stop=True)
                    last.then_inc(s_done, 1)

                def turn(n, h):
                    g = n * S.H + h
                    pe.wait_ge(p_done, g + 3)
                    for half in range(HALVES):
                        pe.wait_ge(t_read_a if half else t_read_v, g + 1)
                        for k in range(BANK // P):
                            c = half * BANK + k * P
                            last = nc.tensor.transpose(bank(PT0 + half)[:, k * P:(k + 1) * P],
                                                       prob[h % 2][:, c:c + P], sb["ident"][:])
                        last.then_inc(t_done, 1)

                def weigh(n, h):
                    g = n * S.H + h
                    pe.wait_ge(t_read_a, g + 2)
                    pe.wait_ge(t_read_v, g + 2)
                    for k in range(S.T):
                        last = nc.tensor.matmul(bank(OB)[:, h * S.D:(h + 1) * S.D], probT[h % 2][:, k, :],
                                                vals[:, k, h * S.D:(h + 1) * S.D],
                                                start=(k == 0), stop=(k == S.T - 1))
                    last.then_inc(pv_done, 1)

                def turn_output(n):
                    pe.wait_ge(o_norm, n + 1)
                    pe.wait_ge(tile_done, n + 1)
                    for k in range(S.F // P):
                        last = nc.tensor.transpose(bank(MB)[:, k * P:(k + 1) * P], o_sb[:, k * P:(k + 1) * P],
                                                   sb["ident"][:])
                    last.then_inc(oT_done, 1)

                def project(n):
                    pe.wait_ge(oT_read, n + 1)
                    for k in range(S.F // P):
                        last = nc.tensor.matmul(bank(MB)[:, 0:S.C], oT[:, k, :], sb["wprojT"][:, k, :],
                                                start=(k == 0), stop=(k == S.F // P - 1))
                    last.then_inc(y_done, 1)

                def tile(n, u, first=False):
                    pe.wait_ge(q_ready, n + 1)
                    scores(n, u, 0)
                    if not first:
                        weigh(n - 1, S.H - 1)
                    for h in range(S.H):
                        if h + 1 < S.H:
                            scores(n, u, h + 1)
                        turn(n, h)
                        if h == 0 and not first:
                            turn_output(n - 1)
                        if h:
                            weigh(n, h - 1)
                        if h == 1 and not first:
                            project(n - 1)

                pe.wait_ge(job_read_a, b * JA + JA)
                pe.wait_ge(job_read_v, b * JV + JV)
                tile(b * S.T, 0, first=True)
                tile(b * S.T + 1, 1)
                with pe.Fori(1, S.T // 2) as i2:
                    for u in range(2):
                        tile(b * S.T + i2 * 2 + u, u)
                weigh(b * S.T + S.T - 1, S.H - 1)
                turn_output(b * S.T + S.T - 1)
                project(b * S.T + S.T - 1)

        @block.scalar
        def _(act):
            act.sem_inc(t_read_a, 1)
            act.sem_inc(p_done, 2)
            with act.Fori(0, S.B) as b:
                for j in range(JOBS):
                    if not by_act(j):
                        continue
                    act.wait_ge(job_done, b * JOBS + j + 1)
                    if j < 4:
                        i = nc.scalar.activation(g0[:, (j - 2) * BANK:(j - 1) * BANK], bank(j), ACT.Exp,
                                                 bias=sb["bgam"][:, 0:1])
                    elif j == 4:
                        i = nc.scalar.activation(g1[:], bank(j)[:, 1:2 * S.T:2], ACT.Exp, bias=sb["bgam"][:, 1:2])
                    elif j < V0:
                        pair, half = divmod(j - K0, HALVES)
                        i = nc.scalar.copy(kT[:, pair, half * BANK:(half + 1) * BANK], bank(j % 8))
                    else:
                        i = nc.scalar.copy(vals[:, j - V0, :], bank(j % 8))
                    i.then_inc(job_read_a, 1)
                with act.Fori(0, S.T // 2) as i2:
                    for u in range(2):
                        n = b * S.T + i2 * 2 + u

                        def exps(h):
                            g = n * S.H + h
                            act.wait_ge(s_read, g + 3)
                            act.wait_ge(t_done, g * 2 + 1)
                            nc.scalar.activation(prob[h % 2][:], neg[h % 2][:], ACT.Exp, scale=-1.0,
                                                 bias=neg_max[u][:, h:h + 1],
                                                 accum_out=row_sum[u][:, h:h + 1]).then_inc(p_done, 1)

                        def evac(h):
                            g = n * S.H + h
                            act.wait_ge(t_done, g * 2 + 2 + 3)
                            act.wait_ge(pv_done, g + 1)
                            nc.scalar.copy(probT[h % 2][:, S.T // 2:, :].rearrange("p t q -> p (t q)"),
                                           bank(PT0 + 1)).then_inc(t_read_a, 1)

                        exps(0)
                        for h in range(S.H):
                            if h + 1 < S.H:
                                exps(h + 1)
                            evac(h)

        @block.vector
        def _(v):
            v.sem_inc(t_read_v, 1)
            v.sem_inc(s_read, 2)
            v.sem_inc(tile_done, 1)
            v.sem_inc(adj_free, 2)
            v.sem_inc(t_done, 3)
            v.sem_inc(pv_done, 2)
            with v.Fori(0, S.B) as b:
                nc.vector.tensor_copy(h_b[:], sb["h"][:, :, bass.ds(b, 1), :].rearrange("p t o c -> p (t o) c")).then_inc(h_ready, 1)
                for j in range(JOBS):
                    if by_act(j):
                        continue
                    v.wait_ge(job_done, b * JOBS + j + 1)
                    if j < 2:
                        i = nc.vector.tensor_copy(hT[:, j * BANK:(j + 1) * BANK], bank(j)[0:S.C, :])
                    elif j < Q0:
                        i = nc.vector.tensor_copy(vals[:, j - V0, :], bank(j % 8))
                    else:
                        pair, half = divmod(j - Q0, HALVES)
                        v.wait_ge(job_read_a, b * JA + n_act(3))
                        i = nc.vector.tensor_tensor(qT_all[:, pair, half * BANK:(half + 1) * BANK], bank(j % 8),
                                                    g0[:, half * BANK:(half + 1) * BANK], ALU.mult)
                    i.then_inc(job_read_v, 1)
                v.wait_ge(job_read_a, b * JA + JA)

                def take_max(n, u, h):
                    g = n * S.H + h
                    v.wait_ge(s_done, g + 1 + 2 * S.H)
                    wait_alone(v, p_done, g + 1, passed)
                    nc.vector.tensor_tensor_reduce(
                        out=neg[h % 2][:], in0=ps[:, 2 * (h % 2) * BANK:(2 * (h % 2) + 2) * BANK],
                        in1=bias_t[u][:], scale=-1.0, scalar=3.0e38, op0=ALU.add, op1=ALU.min,
                        accum_out=neg_max[u][:, h:h + 1]).then_inc(s_read, 1)

                def evac(n, h):
                    g = n * S.H + h
                    v.wait_ge(t_done, g * 2 + 1 + 3)
                    v.wait_ge(pv_done, g + 1)
                    nc.vector.tensor_copy(probT[h % 2][:, 0:S.T // 2, :].rearrange("p t q -> p (t q)"),
                                          bank(PT0)).then_inc(t_read_v, 1)

                def normalise(n, u):
                    v.wait_ge(pv_done, n * S.H + S.H + 2)
                    nc.vector.reciprocal(row_inv[:], row_sum[u][:])
                    v.drain()
                    nc.vector.tensor_tensor(o_sb[:].rearrange("p (h d) -> p h d", d=S.D),
                                            bank(OB).rearrange("p (h d) -> p h d", d=S.D),
                                            row_inv[:, :, None].to_broadcast([P, S.H, S.D]),
                                            ALU.mult).then_inc(o_norm, 1)

                def take_turned(n):
                    v.wait_ge(oT_done, n + 1)
                    nc.vector.tensor_copy(oT[:].rearrange("p k q -> p (k q)"), bank(MB)).then_inc(oT_read, 1)

                def finish(n, i):
                    v.wait_ge(y_done, n + 1)
                    nc.vector.tensor_tensor(y_sb[:], bank(MB)[:, 0:S.C], sb["bproj"][:], ALU.add)
                    v.drain()
                    x1 = sb["x1"][:, bass.ds(i, 1), bass.ds(b, 1), :].rearrange("p t b c -> p (t b c)")
                    nc.vector.tensor_tensor(x1, x1, y_sb[:], ALU.add).then_inc(tile_done, 1)

                def tile(i2, u, first=False):
                    i = i2 * 2 + u
                    n = b * S.T + i
                    v.wait_ge(adj_ready[u], (b * (S.T // 2) + i2) * 16 + 16)
                    nc.vector.tensor_scalar(bias_t[u][:], adj_t[u][:], g1[:, i:i + 1] if isinstance(i, int)
                                            else g1[:, bass.ds(i, 1)], None, ALU.mult).then_inc(adj_free, 1)
                    v.drain()
                    take_max(n, u, 0)
                    for h in range(S.H):
                        if h + 1 < S.H:
                            take_max(n, u, h + 1)
                        if h == 0 and not first:
                            normalise(n - 1, 1 - u)
                        evac(n, h)
                        if h == 0 and not first:
                            take_turned(n - 1)
                        if h == 2 and not first:
                            finish(n - 1, i - 1)

                tile(0, 0, first=True)
                tile(0, 1)
                with v.Fori(1, S.T // 2) as i2:
                    for u in range(2):
                        tile(i2, u)
                normalise(b * S.T + S.T - 1, 1)
                take_turned(b * S.T + S.T - 1)
                finish(b * S.T + S.T - 1, S.T - 1)


def sort_phase(nc, S, d, sb):
    with ExitStack() as ctx:
        buf = lambda n, s, dt=FP32: ctx.enter_context(nc.sbuf_tensor(n, s, dt))
        sem = lambda n: ctx.enter_context(nc.semaphore(n))
        BP = S.B // 2
        tmp = buf("ln_tmp1", [P, S.T * S.B, S.C])
        mean, var, y, t = (buf(f"ln1_{n}", [P, S.T * S.B]) for n in ("mean", "var", "y", "t"))
        keys = [buf(f"keys{i}", [P, BP * S.N]) for i in range(2)]
        ps = ctx.enter_context(nc.psum_tensor("ps_sort", [P, 8 * BANK], FP32))
        normed, turned, copied_v, copied_a, is_sorted, stored = (
            sem(n) for n in ("so_normed", "so_turned", "so_copied_v", "so_copied_a", "so_sorted", "so_stored"))
        block = ctx.enter_context(nc.Block())
        levels = S.N.bit_length() - 1
        STEPS = levels * (levels + 1) // 2
        JOBS = BP * S.N // BANK
        PER = BANK // P

        @block.tensor
        def _(pe):
            pe.wait_ge(normed, 1)
            for j in range(JOBS):
                pair, first = divmod(j * PER, S.T)
                for k in range(PER):
                    last = nc.tensor.transpose(ps[:, j * BANK + k * P:j * BANK + (k + 1) * P],
                                               sb["h"][:, first + k, 2 * pair:2 * pair + 2, :]
                                               .rearrange("p b c -> p (b c)"), sb["ident"][:])
                last.then_inc(turned, 1)

        @block.scalar
        def _(act):
            for j in range(1, JOBS, 2):
                act.wait_ge(turned, j + 1)
                nc.scalar.copy(keys[0][:, j * BANK:(j + 1) * BANK], ps[:, j * BANK:(j + 1) * BANK]).then_inc(copied_a, 1)

        @block.vector
        def _(v):
            layer_norm_relu(nc, sb["x1"][:].rearrange("p t b c -> p (t b) c"), sb["h"][:].rearrange("p t b c -> p (t b) c"),
                            tmp[:], mean[:], var[:], y[:], t[:]).then_inc(normed, 1)
            for j in range(0, JOBS, 2):
                v.wait_ge(turned, j + 1)
                nc.vector.tensor_copy(keys[0][:, j * BANK:(j + 1) * BANK], ps[:, j * BANK:(j + 1) * BANK])
            v.wait_ge(copied_a, JOBS // 2)
            v.drain()
            src, dst = keys
            size = 2
            while size <= S.N:
                a, o = (x[:].rearrange("p (n k) -> p n k", k=size) for x in (src, dst))
                half = size // 2
                lo, hi = a[:, :, 0:half], a[:, :, size - 1:half - 1:-1]
                nc.vector.tensor_tensor(o[:, :, 0:half], lo, hi, ALU.min)
                nc.vector.tensor_tensor(o[:, :, size - 1:half - 1:-1], lo, hi, ALU.max)
                v.drain()
                src, dst = dst, src
                step = size // 4
                while step:
                    a, o = (x[:].rearrange("p (n two k) -> p n two k", two=2, k=step) for x in (src, dst))
                    nc.vector.tensor_tensor(o[:, :, 0, :], a[:, :, 0, :], a[:, :, 1, :], ALU.min)
                    nc.vector.tensor_tensor(o[:, :, 1, :], a[:, :, 0, :], a[:, :, 1, :], ALU.max)
                    v.drain()
                    src, dst = dst, src
                    step //= 2
                size *= 2
            nc.vector.tensor_copy(dst[:], src[:]).then_inc(is_sorted, 1)

        @block.sync
        def _(sp):
            sp.wait_ge(is_sorted, 1)
            for pair in range(BP):
                sp.dma_start(d["sorted"][2 * pair:2 * pair + 2].rearrange("b c n -> (b c) n"),
                             keys[(STEPS + 1) % 2][:, pair * S.N:(pair + 1) * S.N]).then_inc(stored, 16)
            sp.wait_ge(stored, 16 * BP)


SLOTS = (0, 48, 32, 32, 24, 24, 24, 24)


def thin_phase(nc, S, d, sb):
    with ExitStack() as ctx:
        buf = lambda n, s, dt=FP32: ctx.enter_context(nc.sbuf_tensor(n, s, dt))
        sem = lambda n: ctx.enter_context(nc.semaphore(n))
        Q = len(TAUS)
        adj_t = [buf(f"cadj{u}", [P, S.N]) for u in range(2)]
        keep = buf("keep", [P, S.T, S.N], BF16)
        rem = buf("rem", [P, S.T, S.N], BF16)
        rank = buf("rank", [P, S.T, S.N], FP16)
        nearT = buf("tnearT", [P, S.T, S.N], BF16)
        deg, odd, skip, first, second = (buf(n, [P, S.T]) for n in ("deg", "odd", "skip", "first", "second"))
        deg_i = buf("deg_i", [P, S.T], INT32)
        load = buf("load", [P, S.B, S.T])
        top = buf("top", [P, 1])
        top1 = buf("top1", [1, 1])
        ps = ctx.enter_context(nc.psum_tensor("ps_thin", [P, 8 * BANK], FP32))
        bank = lambda k, n=1: ps[:, k * BANK:(k + n) * BANK]
        adj_ready = [sem(f"cadj_ready{u}") for u in range(2)]
        adj_read, near_made, turned, turn_read, near_done, deg_done, deg_read, near_stored, top_done, top_turned, passed = (
            sem(n) for n in ("cadj_read", "near_made", "c_turned", "turn_read", "near_done", "deg_done", "deg_read",
                             "near_stored", "top_done", "top_turned", "tpassed"))
        block = ctx.enter_context(nc.Block())

        @block.sync
        def _(sp):
            sp.sem_inc(near_stored, 16)
            with sp.Fori(0, S.B) as b:
                for k in range(S.T):
                    sp.wait_ge(adj_read, b * S.T + k + 1)
                    sp.dma_start(adj_t[k % 2][:], d["adj"][bass.ds(b, 1), k * P:(k + 1) * P, :]
                                 .rearrange("o p n -> (o p) n")).then_inc(adj_ready[k % 2], 16)
                wait_alone(sp, near_done, b + 1, passed)
                sp.dma_start(d["near"][bass.ds(b, 1)].rearrange("o p n -> (o p) n"),
                             nearT[:].rearrange("p t n -> p (t n)")).then_inc(near_stored, 16)
            sp.wait_ge(near_stored, 16 * S.B + 16)

        @block.tensor
        def _(pe):
            with pe.Fori(0, S.B) as b:
                pe.wait_ge(near_made, b + 1)
                for k in range(S.T):
                    pe.wait_ge(turn_read, b * S.T + k + 1)
                    half = bank(k % 2).bitcast(BF16)
                    for i in range(S.T):
                        last = nc.tensor.transpose(half[:, i * P:(i + 1) * P], keep[:, i, k * P:(k + 1) * P], sb["ident_b"][:])
                    last.then_inc(turned, 1)
                pe.wait_ge(near_done, b + 1)
                pe.wait_ge(deg_read, b + 1)
                for i in range(S.T):
                    for k in range(S.T):
                        last = nc.tensor.matmul(bank(2)[:, i:i + 1], nearT[:, k, i * P:(i + 1) * P], sb["ones_b"][:, 0:1],
                                                start=(k == 0), stop=(k == S.T - 1))
                last.then_inc(deg_done, 1)
            pe.wait_ge(top_done, 1)
            nc.tensor.transpose(bank(3)[0:1, 0:P], top[:], sb["ident"][:]).then_inc(top_turned, 1)

        @block.vector
        def _(v):
            v.sem_inc(adj_read, 2)
            v.sem_inc(turn_read, 2)
            v.sem_inc(deg_read, 1)
            with v.Fori(0, S.B) as b:
                for k in range(S.T):
                    v.wait_ge(adj_ready[k % 2], (b * (S.T // 2) + k // 2) * 16 + 16)
                    nc.vector.tensor_scalar(keep[:, k, :], adj_t[k % 2][:], 0.0, None, ALU.is_gt).then_inc(adj_read, 1)
                    v.drain()
                    own_block = keep[:, k, k * P:(k + 1) * P]
                    nc.vector.tensor_tensor(own_block, own_block, sb["off_diag"][:], ALU.mult)
                    v.drain()
                    nc.vector.tensor_tensor_scan(rank[:, k, :], keep[:, k, :], keep[:, k, :], 0.0, ALU.add, ALU.max)
                v.drain()
                nc.vector.tensor_copy(deg[:], rank[:, :, S.N - 1])
                v.drain()
                nc.vector.tensor_copy(deg_i[:], deg[:])
                v.drain()
                nc.vector.tensor_scalar(deg_i[:], deg_i[:], 1, None, ALU.bitwise_and)
                v.drain()
                nc.vector.tensor_copy(odd[:], deg_i[:])
                v.drain()
                nc.vector.tensor_tensor(skip[:], deg[:], odd[:], ALU.add)
                v.drain()
                nc.vector.tensor_scalar(odd[:], deg[:], DEG_T, None, ALU.is_gt)
                v.drain()
                nc.vector.tensor_tensor(odd[:], odd[:], sb["mask"][:, bass.ds(b * S.T, S.T)], ALU.mult)
                v.drain()
                nc.vector.tensor_tensor(second[:], skip[:], odd[:], ALU.mult)
                v.drain()
                nc.vector.tensor_scalar(first[:], second[:], 0.5, None, ALU.mult)
                v.drain()
                for k in range(S.T):
                    nc.vector.tensor_scalar(rem[:, k, :], rank[:, k, :], first[:, k:k + 1], None, ALU.is_equal)
                v.drain()
                for k in range(S.T):
                    nc.vector.scalar_tensor_tensor(rem[:, k, :], rank[:, k, :], second[:, k:k + 1], rem[:, k, :],
                                                   ALU.is_equal, ALU.add)
                v.drain()
                nc.vector.tensor_tensor(rem[:], rem[:], keep[:], ALU.mult)
                v.drain()
                nc.vector.tensor_tensor(keep[:], keep[:], rem[:], ALU.subtract).then_inc(near_made, 1)
                for k in range(S.T):
                    v.wait_ge(turned, b * S.T + k + 1)
                    v.wait_ge(near_stored, b * 16 + 16)
                    nc.vector.scalar_tensor_tensor(nearT[:, k, :], rem[:, k, :], 0.0, bank(k % 2).bitcast(BF16),
                                                   ALU.is_equal, ALU.mult).then_inc(turn_read, 1)
                    v.drain()
                    own_block = nearT[:, k, k * P:(k + 1) * P]
                    last = nc.vector.tensor_tensor(own_block, own_block, sb["ident_b"][:], ALU.max)
                last.then_inc(near_done, 1)
                v.wait_ge(deg_done, b + 1)
                nc.vector.tensor_copy(sb["deg"][:, bass.ds(b * S.T, S.T)], bank(2)[:, 0:S.T]).then_inc(deg_read, 1)
            v.drain()
            degs = sb["deg"][:].rearrange("p (b t) -> p b t", t=S.T)
            for k in range(S.T):
                nc.vector.tensor_scalar(load[:, :, k], degs[:, :, k], 1.0 / SLOTS[k] if SLOTS[k] else 0.0, None, ALU.mult)
            v.drain()
            nc.vector.reduce_max(top[:], load[:].rearrange("p b t -> p (b t)"), axis=AX.X).then_inc(top_done, 1)
            for q in range(Q):
                nc.vector.tensor_scalar(sb["bias"][:, :, q], sb["deg"][:], WTS[q] * TAUS[q],
                                        WTS[q] * (1.0 - TAUS[q]), ALU.mult, ALU.add)
            v.wait_ge(top_turned, 1)
            nc.vector.reduce_max(top1[:], bank(3)[0:1, 0:P], axis=AX.X)
            v.drain()
            nc.vector.tensor_scalar(sb["fits"][:], top1[:], 1.0, None, ALU.is_le)


def mlp_phase(nc, S, d, sb):
    with ExitStack() as ctx:
        buf = lambda n, s, dt=FP32: ctx.enter_context(nc.sbuf_tensor(n, s, dt))
        sem = lambda n: ctx.enter_context(nc.semaphore(n))
        mix = [buf(f"mix{w}", [P, S.T, S.C]) for w in range(2)]
        res = [buf(f"res{w}", [P, S.T, S.C]) for w in range(2)]
        mixT, hidT = buf("mixT", [S.C, S.N]), buf("hidT", [S.HID, S.N])
        ps = ctx.enter_context(nc.psum_tensor("ps_mlp", [P, 8 * BANK], FP32))
        bank = lambda k, n=1: ps[:, k * BANK:(k + n) * BANK]
        names = ("mix_ready", "mixT_done", "mixT_read", "hid_done", "hid_read", "y_done", "res_done", "mlp_passed")
        mix_ready, mixT_done, mixT_read, hid_done, hid_read, y_done, res_done, passed = (sem(n) for n in names)
        out_stored = [sem(f"out_stored{w}") for w in range(2)]
        block = ctx.enter_context(nc.Block())
        HALVES, B2 = S.N // BANK, S.B // 2

        @block.sync
        def _(sp):
            for w in range(2):
                sp.sem_inc(out_stored[w], 16)
            with sp.Fori(0, B2) as b2:
                for w in range(2):
                    wait_alone(sp, res_done, b2 * 2 + w + 1, passed)
                    sp.dma_start(d["out"][bass.ds(b2 * 2 + w, 1)].rearrange("o (t p) c -> p (o t) c", p=P),
                                 res[w][:]).then_inc(out_stored[w], 16)
            for w in range(2):
                sp.wait_ge(out_stored[w], 16 * B2 + 16)

        @block.tensor
        def _(pe):
            with pe.Fori(0, B2) as b2:
                for w in range(2):
                    b = b2 * 2 + w
                    wait_alone(pe, mix_ready, b + 1, passed)
                    for k in range(S.T):
                        last = nc.tensor.transpose(ps[0:S.C, k * P:(k + 1) * P], mix[w][:, k, :], sb["ident"][:])
                    last.then_inc(mixT_done, 1)
                    pe.wait_ge(mixT_read, b + 1)
                    for half in range(HALVES):
                        last = nc.tensor.matmul(bank(2 + half)[0:S.HID, :], sb["w1"][:],
                                                mixT[:, half * BANK:(half + 1) * BANK], start=True, stop=True)
                    last.then_inc(hid_done, 1)
                    pe.wait_ge(hid_read, b + 1)
                    for k in range(S.T):
                        last = nc.tensor.matmul(bank(4 + w)[:, k * S.C:(k + 1) * S.C], hidT[:, k * P:(k + 1) * P],
                                                sb["w2"][:], start=True, stop=True)
                    last.then_inc(y_done, 1)

        @block.scalar
        def _(act):
            act.sem_inc(mixT_done, 2)
            with act.Fori(0, B2) as b2:
                for w in range(2):
                    b = b2 * 2 + w
                    act.wait_ge(mixT_done, b + 1)
                    nc.scalar.copy(mix[w][:], sb["h"][:, :, bass.ds(b, 1), :].rearrange("p t o c -> p (t o) c"))\
                        .then_inc(mix_ready, 1)
                    act.wait_ge(hid_done, b + 1)
                    nc.scalar.activation(hidT[:], bank(2, 2)[0:S.HID, :], ACT.Relu, bias=sb["b1"][:]).then_inc(hid_read, 1)

        @block.vector
        def _(v):
            with v.Fori(0, B2) as b2:
                for w in range(2):
                    b = b2 * 2 + w
                    v.wait_ge(mixT_done, b + 3)
                    nc.vector.tensor_copy(mixT[:], ps[0:S.C, 0:S.N]).then_inc(mixT_read, 1)
                    v.wait_ge(y_done, b + 1)
                    v.wait_ge(out_stored[w], b2 * 16 + 16)
                    nc.vector.tensor_tensor(res[w][:], bank(4 + w)[:, 0:S.T * S.C].rearrange("p (t c) -> p t c", c=S.C),
                                            sb["b2"][:][:, None, :].to_broadcast([P, S.T, S.C]), ALU.add)
                    v.drain()
                    nc.vector.tensor_tensor(res[w][:], res[w][:], sb["mask"][:, bass.ds(b * S.T, S.T)][:, :, None]
                                            .to_broadcast([P, S.T, S.C]), ALU.mult)
                    v.drain()
                    nc.vector.tensor_tensor(res[w][:], res[w][:], sb["x1"][:, :, bass.ds(b, 1), :]
                                            .rearrange("p t o c -> p (t o) c"), ALU.add).then_inc(res_done, 1)


def counting_program(nc, S, d, sb, B, X):
    Q, CB, HALVES = len(TAUS), 4, S.N // BANK
    ps = B["ps"]
    bank = lambda k, n=1: ps[:, k * BANK:(k + n) * BANK]
    level, gap, below, own, ramp, nearT = (B[n] for n in ("level", "gap", "below", "own", "ramp", "nearT"))
    agg = B["agg"]

    def sync(sp):
        with sp.Fori(0, S.B) as b:
            wait_alone(sp, X["near_free"], b + 1, X["passed"])
            sp.dma_start(nearT[:].rearrange("p t n -> p (t n)"), d["near"][bass.ds(b, 1)]
                         .rearrange("o p n -> (o p) n")).then_inc(X["near_ready"], 16)
            with sp.Fori(0, S.C // 2) as c2:
                for w in range(2):
                    sp.wait_ge(X["below_done"], b * S.C + c2 * 2 + w + 1)
                    sp.dma_start(level[w][:], d["sorted"][bass.ds(b, 1), bass.ds(c2 * 2 + w, 1), :]
                                 .rearrange("o c n -> (o c) n").to_broadcast([P, S.N])).then_inc(X["level_ready"][w], 16)

    def gpsimd(pool):
        pool.sem_inc(X["below_done"], 2)
        with pool.Fori(0, S.B) as b:
            with pool.Fori(0, S.C // 2) as c2:
                for w in range(2):
                    c = b * S.C + c2 * 2 + w
                    pool.wait_ge(X["counted"], (c + 1) * S.T)
                    nc.gpsimd.tensor_copy(own[w][:], sb["h"][:, :, bass.ds(b, 1), bass.ds(c2 * 2 + w, 1)]
                                          .rearrange("p t o c -> p (t o c)")).then_inc(X["own_copied"], 1)
                    pool.wait_ge(X["summed"], (c + 1) * S.T)
                    pool.wait_ge(X["own_copied"], c + 1)
                    wait_alone(pool, X["level_ready"][w], (b * (S.C // 2) + c2) * 16 + 16, X["passed"])
                    for k in range(S.T):
                        nc.gpsimd.tensor_scalar(below[w][:, k, :], level[w][:], own[w][:, k:k + 1], None, ALU.is_gt)
                    nc.gpsimd.tensor_tensor(gap[w][:, 1:], level[w][:, 1:], level[w][:, :-1], ALU.subtract)
                    nc.gpsimd.tensor_copy(gap[w][:, 0:1], level[w][:, 0:1])
                    pool.drain().then_inc(X["below_done"], 1)

    def tensor(pe):
        pe.sem_inc(X["counted"], 2 * S.T)
        with pe.Fori(0, S.B) as b:
            with pe.Fori(0, S.C // 2) as c2:
                pe.wait_ge(X["near_ready"], b * 16 + 16)
                for w in range(2):
                    c = b * S.C + c2 * 2 + w
                    pe.wait_ge(X["below_done"], c + 3)
                    for i in range(S.T):
                        pe.wait_ge(X["ramped"], c * S.T + i + 1)
                        for half in range(HALVES):
                            for k in range(S.T):
                                last = nc.tensor.matmul(bank(2 * (i % CB) + half), nearT[:, k, i * P:(i + 1) * P],
                                                        below[w][:, k, half * BANK:(half + 1) * BANK],
                                                        start=(k == 0), stop=(k == S.T - 1))
                        last.then_inc(X["counted"], 1)

    def scalar(act):
        act.sem_inc(X["ramped"], CB)
        with act.Fori(0, S.B) as b:
            act.drain()
            nc.scalar.copy(B["bias_b"][:], sb["bias"][:, bass.ds(b * S.T, S.T), :])
            act.drain()
            with act.Fori(0, S.C // 2) as c2:
                for w in range(2):
                    for i in range(S.T):
                        g = (b * S.C + c2 * 2 + w) * S.T + i
                        act.wait_ge(X["counted"], g + 1 + 2 * S.T)
                        act.wait_ge(X["summed"], g + S.T * 2 - 1)
                        for q in range(Q):
                            last = nc.scalar.activation(ramp[i % 2][:, q, :], bank(2 * (i % CB), 2), ACT.Relu,
                                                        bias=B["bias_b"][:, i, q:q + 1], scale=-WTS[q])
                        last.then_inc(X["ramped"], 1)

    def vector(v):
        v.sem_inc(X["summed"], 2 * S.T)
        v.sem_inc(X["near_free"], 1)
        with v.Fori(0, S.B) as b:
            with v.Fori(0, S.C // 2) as c2:
                for w in range(2):
                    for i in range(S.T):
                        g = (b * S.C + c2 * 2 + w) * S.T + i
                        v.wait_ge(X["ramped"], g + 1 + CB)
                        for q in range(Q):
                            last = nc.vector.scalar_tensor_tensor(
                                ramp[i % 2][:, q, :], ramp[i % 2][:, q, :], WTS[q], gap[w][:], ALU.min, ALU.mult,
                                accum_out=agg[:, i, q, bass.ds(c2 * 2 + w, 1)])
                        last.then_inc(X["summed"], 1)
            v.drain().then_inc(X["near_free"], 1)
            h_graph = sb["h"][:, :, bass.ds(b, 1), :].rearrange("p t o c -> p (t o) c")
            for q in range(Q):
                nc.vector.tensor_tensor(h_graph, h_graph, agg[:, :, q, :], ALU.add)
                v.drain()

    return dict(sync=sync, gpsimd=gpsimd, tensor=tensor, scalar=scalar, vector=vector)


BIG = 2.0 ** 100
LOG = {2 ** k: k for k in range(11)}


def slots_program(nc, S, d, sb, B, X):
    Q, HALVES = len(TAUS), S.N // BANK
    ps = B["ps"]
    bank = lambda k, n=1: ps[:, k * BANK:(k + n) * BANK]
    level, gap, below, own, ramp, nearT = (B[n] for n in ("level", "gap", "below", "own", "ramp", "nearT"))
    order, near0, vals, tmp, hot, parts, agg0, aggs, own_bias, wts, fit = (
        B[n] for n in ("order", "near0", "vals", "tmp", "hot", "parts", "agg0", "aggs", "own_bias", "wts", "fit"))
    rest = B["rest"]
    FEW = 2
    SHARES = ((2, 1), (3, 1), (0, 2), (0, 2), (0, 2), (1, 2), (1, 2), (1, 2))
    START = (0, 1)
    LV = len(level)
    C4 = S.C // LV
    G = 2
    SB = BANK // S.C
    GROUPS = sum(SLOTS) // G
    BANKS = sum(SLOTS) // SB
    TILES = S.T - 1
    CH = S.C // S.T
    GB = 4
    ALIKE = SLOTS.index(SLOTS[-1])
    slots0 = lambda t, unit: (sum(SLOTS[:t]) // unit if isinstance(t, int) else
                              sum(SLOTS[:ALIKE]) // unit + (t - ALIKE) * (SLOTS[-1] // unit))
    group0 = lambda b, t: b * GROUPS + slots0(t, G)
    bank0 = lambda b, t: b * BANKS + slots0(t, SB)

    def sync(sp):
        with sp.Fori(0, S.B) as b:
            wait_alone(sp, X["order_read"], b * S.T + 2, X["passed"])
            wait_alone(sp, X["near0_copied"], b + 1, X["passed"])
            sp.dma_start(nearT[:].rearrange("p t n -> p (t n)"), d["near"][bass.ds(b, 1)]
                         .rearrange("o p n -> (o p) n")).then_inc(X["near_ready"], 16)
            with sp.Fori(0, C4) as c4:
                for w in range(LV):
                    c = b * S.C + c4 * LV + w
                    sp.wait_ge(X["gap_made"], c + 1)
                    sp.wait_ge(X["below_p"], c + 1)
                    sp.wait_ge(X["below_v"], c + 1)
                    wait_alone(sp, X["below_a"], c + 1, X["passed"])
                    sp.dma_start(level[w][:, 1:], d["sorted"][bass.ds(b, 1), bass.ds(c4 * LV + w, 1), :]
                                 .rearrange("o c n -> (o c) n").to_broadcast([P, S.N])).then_inc(X["level_ready"][w], 16)

    def gpsimd(pool):
        pool.sem_inc(X["below_p"], LV)
        pool.sem_inc(X["gap_made"], LV)

        def levels(b, c4, share):
            for w in range(LV):
                c = b * S.C + c4 * LV + w
                K = S.T - share
                nc.gpsimd.tensor_copy(own[w % 2][:, K:], sb["h"][:, K:, bass.ds(b, 1), bass.ds(c4 * LV + w, 1)]
                                      .rearrange("p t o c -> p (t o c)")).then_inc(X["own_copied"], 1)
                pool.wait_ge(X["counted"], c + 1)
                pool.wait_ge(X["own_copied"], c + 1)
                wait_alone(pool, X["level_ready"][w], (b * C4 + c4) * 16 + 16, X["passed"])
                for k in range(K, S.T):
                    last = nc.gpsimd.tensor_scalar(below[w % 2][:, k, :], level[w][:, 1:], own[w % 2][:, k:k + 1],
                                                   None, ALU.is_gt)
                last.then_inc(X["below_p"], 1)
                pool.wait_ge(X["summed"], c + 1)
                nc.gpsimd.tensor_tensor(gap[w % 2][:], level[w][:, 1:], level[w][:, :-1], ALU.subtract)\
                    .then_inc(X["gap_made"], 1)

        for w in range(LV):
            nc.gpsimd.memset(level[w][:, 0:1], 0.0)
        with pool.Fori(0, S.B) as b:
            with pool.Fori(0, FEW * CH // LV) as c4:
                levels(b, c4, SHARES[0][1])
            with pool.Fori(FEW * CH // LV, C4) as c4:
                levels(b, c4, SHARES[FEW][1])

    def tensor(pe):
        pe.sem_inc(X["counted"], 2)
        pe.sem_inc(X["hot_used"], 2)

        def count(c, w):
            for name in ("below_p", "below_v", "below_a"):
                pe.wait_ge(X[name], c + 1 + LV)
            pe.wait_ge(X["ramped"], c + 1)
            for half in range(HALVES):
                for k in range(S.T):
                    last = nc.tensor.matmul(bank(2 * w + half), near0[:, k, :],
                                            below[w][:, k, half * BANK:(half + 1) * BANK],
                                            start=(k == 0), stop=(k == S.T - 1))
            last.then_inc(X["counted"], 1)

        def gather(g0, v0, g):
            s = g * G
            pe.wait_ge(X["hot_done"], g0 + g + 1)
            if s % SB == 0:
                pe.wait_ge(X["vals_read"], v0 + 4 + max(s // SB - 3, 0))
            for u in range(G):
                o = bank(GB + s // SB % 4)[:, (s % SB + u) * S.C:(s % SB + u + 1) * S.C]
                for k in range(S.T):
                    for part in range(3):
                        last = nc.tensor.matmul(o, hot[g % 2][:, u, k, :], parts[:, k, part, :],
                                                start=(k == 0 and part == 0), stop=(k == S.T - 1 and part == 2))
            last.then_inc(X["hot_used"], 1)

        def make_order(b, k):
            pe.wait_ge(X["order_read"], b * S.T + k + 1)
            for half in range(HALVES):
                for j in range(k + 1):
                    last = nc.tensor.matmul(bank(GB + 2 * (k % 2) + half), (sb["ones_b"] if j < k else sb["upto_b"])[:],
                                            nearT[:, j, half * BANK:(half + 1) * BANK],
                                            start=(j == 0), stop=(j == k))
            last.then_inc(X["order_done"], 1)

        def block(b, cb, t):
            groups = SLOTS[t if isinstance(t, int) else -1] // G
            for j in range(CH):
                count(b * S.C + cb * CH + j, j % 2)
                for g in range(groups * j // CH, groups * (j + 1) // CH):
                    gather(group0(b, t), bank0(b, t), g)

        with pe.Fori(0, S.B) as b:
            pe.wait_ge(X["near_ready"], b * 16 + 16)
            pe.wait_ge(X["vals_read"], b * BANKS + 4)
            make_order(b, 0)
            make_order(b, 1)
            pe.wait_ge(X["near0_copied"], b + 2)
            for j in range(CH):
                count(b * S.C + j, j % 2)
                if j + 2 < S.T:
                    make_order(b, j + 2)
            for t in range(1, ALIKE + 1):
                block(b, t, t)
            with pe.Fori(ALIKE + 1, S.T) as t:
                block(b, t, t)

    def scalar(act):
        act.sem_inc(X["below_a"], LV)
        act.sem_inc(X["ramped"], 2)
        act.sem_inc(X["near0_copied"], 1)
        act.sem_inc(X["vals_read"], 4)

        def compare(b, c4, w, share):
            c = b * S.C + c4 * LV + w
            act.wait_ge(X["counted"], c + 1)
            act.wait_ge(X["level_ready"][w], (b * C4 + c4) * 16 + 16)
            for k in range(share[0], S.T - share[1]):
                last = nc.scalar.activation(below[w % 2][:, k, :], level[w][:, 1:], ACT.Sigmoid,
                                            bias=own_bias[:, k, bass.ds(b, 1), bass.ds(c4 * LV + w, 1)]
                                            .rearrange("p o c -> p (o c)"), scale=BIG)
            last.then_inc(X["below_a"], 1)

        def ramps(b, c4, w):
            c = b * S.C + c4 * LV + w
            act.wait_ge(X["counted"], c + 3)
            act.wait_ge(X["summed"], c + 1)
            for q in range(Q):
                last = nc.scalar.activation(ramp[w % 2][:, q, :], bank(2 * (w % 2), 2), ACT.Relu,
                                            bias=B["bias_b"][:, 0, q:q + 1], scale=-WTS[q])
            last.then_inc(X["ramped"], 1)

        def take(g0, v_free, k):
            act.wait_ge(X["hot_used"], g0 + (k + 1) * (SB // G) + 2)
            act.wait_ge(X["vals_free"], v_free)
            nc.scalar.copy(vals[:, k * SB * S.C:(k + 1) * SB * S.C], bank(GB + k % 4)).then_inc(X["vals_read"], 1)

        def block(b, cb, shares, t=None):
            slots = 0 if t is None else SLOTS[t if isinstance(t, int) else -1]
            early = isinstance(t, int) and t == 1
            filled = lambda j: slots // G * j // CH // (SB // G)
            for j in range(CH):
                if j + 1 < CH or len(shares) > 1:
                    compare(b, cb * (CH // LV) + (j + 1) // LV, (j + 1) % LV, shares[(j + 1) // CH])
                ramps(b, cb * (CH // LV) + j // LV, j % LV)
                if early:
                    for k in range(filled(j), filled(j + 1)):
                        take(group0(b, t), b * TILES + t, k)
            if not early:
                for k in range(slots // SB):
                    take(group0(b, t), b * TILES + t, k)

        act.wait_ge(X["bias_made"], 1)
        with act.Fori(0, S.B) as b:
            act.wait_ge(X["near_ready"], b * 16 + 16)
            act.wait_ge(X["near_free"], b + 1)
            nc.scalar.copy(B["bias_b"][:], sb["bias"][:, bass.ds(b * S.T, S.T), :])
            nc.scalar.copy(near0[:], nearT[:, :, 0:P]).then_inc(X["near0_copied"], 1)
            compare(b, 0, 0, START)
            block(b, 0, SHARES[0:2])
            for t in range(1, ALIKE + 1):
                block(b, t, SHARES[t:t + 2], t)
            with act.Fori(ALIKE + 1, S.T - 1) as t:
                block(b, t, SHARES[-2:], t)
            block(b, S.T - 1, SHARES[-1:], S.T - 1)

    def vector(v):
        v.sem_inc(X["below_v"], LV)
        v.sem_inc(X["summed"], 2)
        v.sem_inc(X["near_free"], 1)
        v.sem_inc(X["order_read"], 2)
        v.sem_inc(X["vals_free"], 1)

        def compare(b, c4, w, share):
            c = b * S.C + c4 * LV + w
            if not share[0]:
                v.sem_inc(X["below_v"], 1)
                return
            v.wait_ge(X["counted"], c + 1)
            v.wait_ge(X["level_ready"][w], (b * C4 + c4) * 16 + 16)
            for k in range(share[0]):
                last = nc.vector.tensor_scalar(below[w % 2][:, k, :], level[w][:, 1:],
                                               sb["h"][:, k, bass.ds(b, 1), bass.ds(c4 * LV + w, 1)]
                                               .rearrange("p o c -> p (o c)"), None, ALU.is_gt)
            last.then_inc(X["below_v"], 1)

        def sums(b, c4, w):
            c = b * S.C + c4 * LV + w
            v.wait_ge(X["ramped"], c + 3)
            v.wait_ge(X["gap_made"], c + 1 + LV)
            for q in range(Q):
                last = nc.vector.scalar_tensor_tensor(
                    ramp[w % 2][:, q, :], ramp[w % 2][:, q, :], WTS[q], gap[w % 2][:], ALU.min, ALU.mult,
                    accum_out=agg0[:, q, bass.ds(c4 * LV + w, 1)])
            last.then_inc(X["summed"], 1)

        def one_hot(base, t, g):
            v.wait_ge(X["hot_used"], base + g + 1)
            for u in range(G):
                last = nc.vector.tensor_scalar(hot[g % 2][:, u, :, :], order[:, :, bass.ds(t * P, P)],
                                               float(g * G + u + 1), None, ALU.is_equal)
            last.then_inc(X["hot_done"], 1)

        def between(b, cb, shares, t, i, n):
            groups = 0 if t is None else SLOTS[t if isinstance(t, int) else -1] // G
            for j in range(CH * i // n, CH * (i + 1) // n):
                for g in range(groups * j // CH, groups * (j + 1) // CH):
                    one_hot(group0(b, t), t, g)
                if j + 1 < CH or len(shares) > 1:
                    compare(b, cb * (CH // LV) + (j + 1) // LV, (j + 1) % LV, shares[(j + 1) // CH])
                sums(b, cb * (CH // LV) + j // LV, j % LV)

        def sort(b, t, shares):
            slots = SLOTS[t if isinstance(t, int) else -1]
            v.wait_ge(X["vals_read"], bank0(b, t) + slots // SB + 4)
            C = S.C
            src, dst = vals, tmp
            full = 1 << (slots - 1).bit_length()
            pad = full - slots
            steps, i, size = LOG[full] * (LOG[full] + 1) // 2, 0, 2
            while size <= full:
                half, step = size // 2, size // 2
                while step:
                    first, end = 0, slots
                    if pad and size == full // 2:
                        first = slots - size
                    elif pad and size == full and step == half:
                        end = slots - pad
                    elif pad and size == full and step == pad:
                        first = pad
                    a, o = (x[:, first * C:end * C] for x in (src, dst))
                    if step == half:
                        k = min(size, end - first)
                        a, o = (x.rearrange("p (n k c) -> p n k c", k=k, c=C) for x in (a, o))
                        lo, hi = a[:, :, 0:k // 2, :], a[:, :, k - 1:k // 2 - 1:-1, :]
                        o_lo, o_hi = o[:, :, 0:k // 2, :], o[:, :, k - 1:k // 2 - 1:-1, :]
                    else:
                        a, o = (x.rearrange("p (n two k) -> p n two k", two=2, k=step * C) for x in (a, o))
                        lo, hi, o_lo, o_hi = a[:, :, 0, :], a[:, :, 1, :], o[:, :, 0, :], o[:, :, 1, :]
                    nc.vector.tensor_tensor(o_lo, lo, hi, ALU.min)
                    nc.vector.tensor_tensor(o_hi, lo, hi, ALU.max)
                    if size == full or (step == half and LOG[size] % 2):
                        for s0, s1 in ((0, first), (end, slots)):
                            if s0 < s1:
                                nc.vector.tensor_copy(dst[:, s0 * C:s1 * C], src[:, s0 * C:s1 * C])
                    if shares:
                        between(b, t + 1, shares, t + 1, i, steps)
                    v.drain()
                    src, dst = dst, src
                    step, i = step // 2, i + 1
                size *= 2
            src, dst = src[:, 0:slots * C], dst[:, 0:slots * C]
            w = wts[:, bass.ds(t, 1), 0:slots].rearrange("p o s -> p (o s)")
            nc.vector.tensor_tensor(dst.rearrange("p (s c) -> p s c", c=C), src.rearrange("p (s c) -> p s c", c=C),
                                    w[:, :, None].to_broadcast([P, slots, C]), ALU.mult)
            v.drain()
            nc.vector.reduce_sum(aggs[:, bass.ds(t, 1), :].rearrange("p o c -> p (o c)"),
                                 dst.rearrange("p (s c) -> p c s", c=C), axis=AX.X).then_inc(X["vals_free"], 1)

        for k in range(1, S.T):
            nc.vector.memset(fit[:, k:k + 1], float(SLOTS[k]))
        nc.vector.memset(fit[:, 0:1], float(SLOTS[-1]))
        nc.vector.tensor_scalar(own_bias[:], sb["h"][:], 1.0 + 2.0 ** -23, 1.0 / BIG, ALU.mult, ALU.max)
        v.drain()
        nc.vector.tensor_scalar(own_bias[:], own_bias[:], -BIG, None, ALU.mult).then_inc(X["bias_made"], 1)
        compare(0, 0, 0, START)
        with v.Fori(0, S.B) as b:
            hb = sb["h"][:, :, bass.ds(b, 1), :].rearrange("p t o c -> p (t o) c")
            nc.vector.tensor_copy(parts[:, :, 0, :], hb)
            v.drain()
            nc.vector.tensor_tensor(rest[:], hb, parts[:, :, 0, :], ALU.subtract)
            v.drain()
            nc.vector.tensor_copy(parts[:, :, 1, :], rest[:])
            v.drain()
            nc.vector.tensor_tensor(rest[:], rest[:], parts[:, :, 1, :], ALU.subtract)
            v.drain()
            nc.vector.tensor_copy(parts[:, :, 2, :], rest[:])
            n = sb["deg"][:, bass.ds(b * S.T, S.T)]
            at, off, off2 = B["at"], B["off"], B["off2"]
            for q in range(Q):
                v.drain()
                nc.vector.tensor_scalar(at[:], n, TAUS[q] - 1.0, -TAUS[q], ALU.mult, ALU.add)
                v.drain()
                nc.vector.tensor_tensor(at[:], at[:], fit[:], ALU.add)
                v.drain()
                nc.vector.tensor_tensor(off[:], sb["slot"][:][:, None, :].to_broadcast([P, S.T, max(SLOTS)]),
                                        at[:][:, :, None].to_broadcast([P, S.T, max(SLOTS)]), ALU.subtract)
                v.drain()
                nc.vector.tensor_scalar(off2[:], off[:], -1.0, None, ALU.mult)
                v.drain()
                nc.vector.tensor_tensor(off[:], off[:], off2[:], ALU.min)
                v.drain()
                nc.vector.tensor_scalar(off[:], off[:], 1.0, 0.0, ALU.add, ALU.max)
                v.drain()
                if q == 0:
                    nc.vector.tensor_scalar(wts[:], off[:], WTS[q], None, ALU.mult)
                else:
                    nc.vector.scalar_tensor_tensor(wts[:], off[:], WTS[q], wts[:], ALU.mult, ALU.add)
            for k in range(S.T):
                v.wait_ge(X["order_done"], b * S.T + k + 1)
                nc.vector.tensor_tensor(order[:, k, :], bank(GB + 2 * (k % 2), 2), nearT[:, k, :], ALU.mult)\
                    .then_inc(X["order_read"], 1)
                between(b, 0, SHARES[0:2], None, k, S.T)
            v.drain()
            between(b, 1, SHARES[1:3], 1, 0, 1)
            for t in range(1, ALIKE):
                sort(b, t, SHARES[t + 1:t + 3])
            with v.Fori(ALIKE, S.T - 2) as t:
                sort(b, t, SHARES[-2:])
            sort(b, S.T - 2, SHARES[-1:])
            v.drain().then_inc(X["near_free"], 1)
            compare(b, 0, 0, START)
            sort(b, S.T - 1, None)
            v.drain()
            nc.vector.tensor_tensor(aggs[:, 0, :], agg0[:, 0, :], agg0[:, 1, :], ALU.add)
            v.drain()
            nc.vector.tensor_tensor(aggs[:, 0, :], aggs[:, 0, :], agg0[:, 2, :], ALU.add)
            v.drain()
            nc.vector.tensor_tensor(hb, hb, aggs[:], ALU.add)

    return dict(sync=sync, gpsimd=gpsimd, tensor=tensor, scalar=scalar, vector=vector)


def aggregate_phase(nc, S, d, sb):
    with ExitStack() as ctx:
        buf = lambda n, s, dt=FP32: ctx.enter_context(nc.sbuf_tensor(n, s, dt))
        sem = lambda n: ctx.enter_context(nc.semaphore(n))
        Q, D1 = len(TAUS), max(SLOTS)
        B = dict(
            nearT=buf("nearT", [P, S.T, S.N], BF16),
            gap=[buf(f"gap{w}", [P, S.N]) for w in range(2)],
            below=[buf(f"below{w}", [P, S.T, S.N], BF16) for w in range(2)],
            own=[buf(f"own{w}", [P, S.T]) for w in range(2)],
            ramp=[buf(f"ramp{w}", [P, Q, S.N], BF16) for w in range(2)],
            bias_b=buf("bias_b", [P, S.T, Q]),
            ps=ctx.enter_context(nc.psum_tensor("ps_agg", [P, 8 * BANK], FP32)),
        )
        counting, slots = dict(B), dict(B)
        with ExitStack() as other:
            counting["level"] = [other.enter_context(nc.sbuf_tensor(f"level{w}", [P, S.N], FP32)) for w in range(2)]
            counting["agg"] = other.enter_context(nc.sbuf_tensor("agg", [P, S.T, Q, S.C], FP32))
        slots.update(
            level=[buf(f"slevel{w}", [P, S.N + 1]) for w in range(4)],
            order=buf("order", [P, S.T, S.N], FP16),
            near0=buf("near0", [P, S.T, P], BF16),
            vals=buf("vals_s", [P, D1 * S.C]), tmp=buf("tmp_s", [P, D1 * S.C]),
            hot=[buf(f"hot{u}", [P, 2, S.T, P], BF16) for u in range(2)],
            parts=buf("parts", [P, S.T, 3, S.C], BF16), rest=buf("rest", [P, S.T, S.C]),
            agg0=buf("agg0", [P, Q, S.C]), aggs=buf("aggs", [P, S.T, S.C]),
            own_bias=buf("own_bias", [P, S.T, S.B, S.C]),
            wts=buf("wts", [P, S.T, D1]), fit=buf("fit", [P, S.T]), at=buf("at", [P, S.T]),
            off=buf("off", [P, S.T, D1]), off2=buf("off2", [P, S.T, D1]),
        )
        both = ("near_ready", "near_free", "counted", "ramped", "summed", "own_copied", "passed")
        XC = {n: sem("cnt_" + n) for n in both + ("below_done",)}
        XS = {n: sem("slt_" + n) for n in both + ("near0_copied", "gap_made", "below_p", "below_v", "below_a", "bias_made", "order_done", "order_read",
                                                  "hot_done", "hot_used", "vals_read", "vals_free")}
        XC["level_ready"] = [sem(f"cnt_level_ready{w}") for w in range(2)]
        XS["level_ready"] = [sem(f"slt_level_ready{w}") for w in range(4)]
        by_counting = counting_program(nc, S, d, sb, counting, XC)
        by_slots = slots_program(nc, S, d, sb, slots, XS)
        block = ctx.enter_context(nc.Block())

        def either(eng, name):
            fits = eng.value_load(sb["fits"][0:1, 0:1], min_val=0, max_val=1)
            with eng.If(fits > 0):
                by_slots[name](eng)
            with eng.Else():
                by_counting[name](eng)

        @block.sync
        def _(sp):
            either(sp, "sync")

        @block.gpsimd
        def _(pool):
            either(pool, "gpsimd")

        @block.tensor
        def _(pe):
            either(pe, "tensor")

        @block.scalar
        def _(act):
            either(act, "scalar")

        @block.vector
        def _(v):
            either(v, "vector")


def build(nc, x, adj, mask, w_qkv, w_proj, b_proj, w_gamma, b_gamma, w1, b1, w2, b2, out):
    S = Shapes(x, w_qkv, w1)
    d = dict(x=x, adj=adj, mask=mask, w_qkv=w_qkv, w_proj=w_proj, b_proj=b_proj, w_gamma=w_gamma,
             b_gamma=b_gamma, w1=w1, b1=b1, w2=w2, b2=b2, out=out)
    d["near"] = nc.dram_tensor("near_adjacency", [S.B, P, S.T * S.N], BF16).ap()
    d["sorted"] = nc.dram_tensor("sorted_levels", [S.B, S.C, S.N], FP32).ap()
    with ExitStack() as ctx:
        sb = {}
        for name, shape, dt in (
            ("x1", [P, S.T, S.B, S.C], FP32),
            ("h", [P, S.T, S.B, S.C], FP32),
            ("ident", [P, P], FP32), ("ones", [P, P], FP32), ("off_diag", [P, P], FP32),
            ("ident_b", [P, P], BF16), ("ones_b", [P, P], BF16), ("upto_b", [P, P], BF16),
            ("slot", [P, max(SLOTS)], FP32),
            ("deg", [P, S.B * S.T], FP32),
            ("bias", [P, S.B * S.T, len(TAUS)], FP32),
            ("fits", [1, 1], INT32),
            ("wqkvT", [S.C, 3 * S.F], FP32), ("wprojT", [P, S.F // P, S.C], FP32),
            ("wgam", [S.C, 2], FP32), ("wgam0", [S.C, P], FP32), ("bgam", [P, 2], FP32), ("bproj", [P, S.C], FP32),
            ("w1", [S.C, S.HID], FP32), ("b1", [S.HID, 1], FP32), ("w2", [S.HID, S.C], FP32), ("b2", [P, S.C], FP32),
            ("mask", [P, S.B * S.T], FP32),
        ):
            sb[name] = ctx.enter_context(nc.sbuf_tensor("k_" + name, shape, dt))
        setup_phase(nc, S, d, sb)
        attention_phase(nc, S, d, sb)
        sort_phase(nc, S, d, sb)
        thin_phase(nc, S, d, sb)
        aggregate_phase(nc, S, d, sb)
        mlp_phase(nc, S, d, sb)


_INS = ["x", "adj", "nodemask", "L0_gnn_W_qkv", "L0_gnn_W_proj", "L0_gnn_b_proj", "L0_gnn_W_gamma", "L0_gnn_b_gamma",
        "L1_gnn_W1", "L1_gnn_b1", "L1_gnn_W2", "L1_gnn_b2"]


def kernel(**inputs):
    import numpy as np
    import concourse.bacc as bacc
    from concourse.bass_utils import run_bass_kernel_spmd

    nc = bacc.Bacc("TRN2", target_bir_lowering=False, num_devices=1)
    arrays, args = {}, []
    for name in _INS:
        a = np.ascontiguousarray(inputs[name])
        if a.dtype == np.bool_:
            a = a.view(np.uint8)
        arrays[f"in_{name}"] = a
        args.append(nc.dram_tensor(f"in_{name}", a.shape, mybir.dt.from_np(a.dtype), kind="ExternalInput").ap())
    shape = tuple(np.shape(inputs["x"]))
    out = nc.dram_tensor("out_x", shape, FP32, kind="ExternalOutput").ap()
    build(nc, *args, out)
    r = run_bass_kernel_spmd(nc, [arrays], core_ids=[0])
    return r.results[0]["out_x"]
```
